# Optimizing a Trainium2 kernel written in Bass

```python
import numpy as np
import jax
import jax.numpy as jnp

def _softmax(x, axis=-1):
    return jax.nn.softmax(x, axis=axis)

def _gelu(x):
    return jax.nn.gelu(x, approximate=True)

def _silu(x):
    return jax.nn.silu(x)

def _sigmoid(x):
    return jax.nn.sigmoid(x)

def _layernorm(x, axis=-1, eps=1e-05):
    m = jnp.mean(x, axis=axis, keepdims=True)
    v = jnp.var(x, axis=axis, keepdims=True)
    return (x - m) / jnp.sqrt(v + eps)

def _scatter_add(tgt, idx, src, axis=0):
    return tgt.at[idx].add(src)

def _segment_sum(src, seg, n):
    return jax.ops.segment_sum(src, seg, n)
kernel_name = 'mk_prb_d1_jaxref_r8_bf7ebf'

def setup_inputs(seed: int=0):
    np.random.seed(seed)
    _w = jnp.asarray

    def _L0_attn_setup():
        import jax, jax.numpy as jnp
        import numpy as np
        DIM = 256
        STATE = 64
        DT_RANK = 128
        CHUNK = 64
        key = jax.random.key(seed)
        ks = jax.random.split(key, 8)
        B, L, D, N, R = (4, 256, DIM, STATE, DT_RANK)
        x = jax.random.normal(ks[0], (B, L, D), dtype=jnp.float32)
        norm_w = jnp.ones((D,), jnp.float32)
        norm_b = jnp.zeros((D,), jnp.float32)
        x_proj_w = jax.random.normal(ks[1], (R + 2 * N, D), jnp.float32) * (1.0 / np.sqrt(D))
        dt_proj_w = jax.random.normal(ks[2], (D, R), jnp.float32) * (1.0 / np.sqrt(R))
        dt_proj_b = jax.random.normal(ks[3], (D,), jnp.float32) * 0.01
        A_log = jnp.log(jnp.tile(jnp.arange(1, N + 1, dtype=jnp.float32)[None, :], (D, 1)))
        D_param = jnp.ones((D,), jnp.float32)
        out_proj_w = jax.random.normal(ks[4], (D, D), jnp.float32) * (1.0 / np.sqrt(D))
        return {'x': x, 'norm_w': norm_w, 'norm_b': norm_b, 'x_proj_w': x_proj_w, 'dt_proj_w': dt_proj_w, 'dt_proj_b': dt_proj_b, 'A_log': A_log, 'D_param': D_param, 'out_proj_w': out_proj_w}
    _L0_attn_in = _L0_attn_setup()

    def _L0_ffn_setup():
        import jax, jax.numpy as jnp
        import numpy as np
        from jax import lax
        HIDDEN = 256
        N_EXPERTS = 64
        TOP_K = 6
        N_GROUP = 8
        TOPK_GROUP = 4
        MOE_INTER = 128
        SHARED_INTER = 512
        ROUTED_SCALE = 2.5

        def relu2(x):
            r = jax.nn.relu(x)
            return r * r

        def _route(x2d, gate_w, gate_bias):
            T = x2d.shape[0]
            logits = jnp.einsum('th,eh->te', x2d.astype(jnp.float32), gate_w.astype(jnp.float32))
            scores = jax.nn.sigmoid(logits)
            scores_b = scores + gate_bias[None, :]
            grp = scores_b.reshape(T, N_GROUP, N_EXPERTS // N_GROUP)
            grp_score = lax.top_k(grp, 2)[0].sum(axis=-1)
            _, gidx = lax.top_k(grp_score, TOPK_GROUP)
            gmask = jax.nn.one_hot(gidx, N_GROUP, dtype=jnp.float32).sum(axis=1)
            emask = jnp.repeat(gmask, N_EXPERTS // N_GROUP, axis=1)
            masked = jnp.where(emask > 0, scores_b, -jnp.inf)
            _, eidx = lax.top_k(masked, TOP_K)
            w = jnp.take_along_axis(scores, eidx, axis=1)
            w = w / (w.sum(axis=-1, keepdims=True) + 1e-20) * ROUTED_SCALE
            route_w = jnp.zeros((T, N_EXPERTS), jnp.float32).at[jnp.arange(T)[:, None], eidx].set(w)
            return route_w
        key = jax.random.key(seed)
        ks = jax.random.split(key, 7)
        s_h = 1.0 / np.sqrt(HIDDEN)
        s_i = 1.0 / np.sqrt(MOE_INTER)
        s_s = 1.0 / np.sqrt(SHARED_INTER)
        return {'hidden_states': jax.random.normal(ks[0], (2, 64, HIDDEN), jnp.float32), 'gate_w': jax.random.normal(ks[1], (N_EXPERTS, HIDDEN), jnp.float32) * s_h, 'gate_bias': jax.random.normal(ks[2], (N_EXPERTS,), jnp.float32) * 0.1, 'w_up_shared': jax.random.normal(ks[3], (HIDDEN, SHARED_INTER), jnp.float32) * s_h, 'w_down_shared': jax.random.normal(ks[4], (SHARED_INTER, HIDDEN), jnp.float32) * s_s, 'w1_experts': jax.random.normal(ks[5], (N_EXPERTS, HIDDEN, MOE_INTER), jnp.float32) * s_h, 'w2_experts': jax.random.normal(ks[6], (N_EXPERTS, MOE_INTER, HIDDEN), jnp.float32) * s_i}
    _L0_ffn_in = _L0_ffn_setup()
    _d = {'L0_attn_x': _L0_attn_in['x'], 'L0_attn_norm_w': _L0_attn_in['norm_w'], 'L0_attn_norm_b': _L0_attn_in['norm_b'], 'L0_attn_x_proj_w': _L0_attn_in['x_proj_w'], 'L0_attn_dt_proj_w': _L0_attn_in['dt_proj_w'], 'L0_attn_dt_proj_b': _L0_attn_in['dt_proj_b'], 'L0_attn_A_log': _L0_attn_in['A_log'], 'L0_attn_D_param': _L0_attn_in['D_param'], 'L0_attn_out_proj_w': _L0_attn_in['out_proj_w'], 'L0_ffn_gate_w': _L0_ffn_in['gate_w'], 'L0_ffn_gate_bias': _L0_ffn_in['gate_bias'], 'L0_ffn_w_up_shared': _L0_ffn_in['w_up_shared'], 'L0_ffn_w_down_shared': _L0_ffn_in['w_down_shared'], 'L0_ffn_w1_experts': _L0_ffn_in['w1_experts'], 'L0_ffn_w2_experts': _L0_ffn_in['w2_experts']}
    _x0 = _d['L0_attn_x']
    _d['L0_attn_x'] = jax.random.normal(jax.random.fold_in(jax.random.key(seed), 1), (2, 1024, 256), dtype=_x0.dtype)
    del _x0
    return _d

def reference(L0_attn_x, L0_attn_norm_w, L0_attn_norm_b, L0_attn_x_proj_w, L0_attn_dt_proj_w, L0_attn_dt_proj_b, L0_attn_A_log, L0_attn_D_param, L0_attn_out_proj_w, L0_ffn_gate_w, L0_ffn_gate_bias, L0_ffn_w_up_shared, L0_ffn_w_down_shared, L0_ffn_w1_experts, L0_ffn_w2_experts):

    def _L0_attn_ref(x, norm_w, norm_b, x_proj_w, dt_proj_w, dt_proj_b, A_log, D_param, out_proj_w):
        import jax, jax.numpy as jnp
        import numpy as np
        DIM = 256
        STATE = 64
        DT_RANK = 128
        CHUNK = 64
        B, L, D = x.shape
        N = STATE
        mu = jnp.mean(x, axis=-1, keepdims=True)
        var = jnp.var(x, axis=-1, keepdims=True)
        xn = (x - mu) / jnp.sqrt(var + 1e-05) * norm_w + norm_b
        proj = xn @ x_proj_w.T
        R = dt_proj_w.shape[1]
        delta, B_ssm, C_ssm = jnp.split(proj, [R, R + N], axis=-1)
        delta = jax.nn.softplus(delta @ dt_proj_w.T + dt_proj_b)
        A = -jnp.exp(A_log)
        c_idx = jnp.arange(L) % CHUNK
        C_used = C_ssm[:, c_idx, :]

        def step(h, inp):
            dt, b, xt, c = inp
            dA = jnp.exp(dt[:, :, None] * A)
            h = dA * h + dt[:, :, None] * b[:, None, :] * xt[:, :, None]
            y = jnp.einsum('bdn,bn->bd', h, c)
            return (h, y)
        h0 = jnp.zeros((B, D, N), x.dtype)
        xs = (jnp.moveaxis(delta, 1, 0), jnp.moveaxis(B_ssm, 1, 0), jnp.moveaxis(xn, 1, 0), jnp.moveaxis(C_used, 1, 0))
        _, ys = jax.lax.scan(step, h0, xs)
        y = jnp.moveaxis(ys, 0, 1)
        return (y + x * D_param) @ out_proj_w.T

    def _L0_ffn_ref(hidden_states, gate_w, gate_bias, w_up_shared, w_down_shared, w1_experts, w2_experts):
        import jax, jax.numpy as jnp
        import numpy as np
        from jax import lax
        HIDDEN = 256
        N_EXPERTS = 64
        TOP_K = 6
        N_GROUP = 8
        TOPK_GROUP = 4
        MOE_INTER = 128
        SHARED_INTER = 512
        ROUTED_SCALE = 2.5

        def relu2(x):
            r = jax.nn.relu(x)
            return r * r

        def _route(x2d, gate_w, gate_bias):
            T = x2d.shape[0]
            logits = jnp.einsum('th,eh->te', x2d.astype(jnp.float32), gate_w.astype(jnp.float32))
            scores = jax.nn.sigmoid(logits)
            scores_b = scores + gate_bias[None, :]
            grp = scores_b.reshape(T, N_GROUP, N_EXPERTS // N_GROUP)
            grp_score = lax.top_k(grp, 2)[0].sum(axis=-1)
            _, gidx = lax.top_k(grp_score, TOPK_GROUP)
            gmask = jax.nn.one_hot(gidx, N_GROUP, dtype=jnp.float32).sum(axis=1)
            emask = jnp.repeat(gmask, N_EXPERTS // N_GROUP, axis=1)
            masked = jnp.where(emask > 0, scores_b, -jnp.inf)
            _, eidx = lax.top_k(masked, TOP_K)
            w = jnp.take_along_axis(scores, eidx, axis=1)
            w = w / (w.sum(axis=-1, keepdims=True) + 1e-20) * ROUTED_SCALE
            route_w = jnp.zeros((T, N_EXPERTS), jnp.float32).at[jnp.arange(T)[:, None], eidx].set(w)
            return route_w
        orig_shape = hidden_states.shape
        x2d = hidden_states.reshape(-1, HIDDEN)
        shared = jnp.einsum('ti,ih->th', relu2(jnp.einsum('th,hi->ti', x2d, w_up_shared)), w_down_shared)
        route_w = _route(x2d, gate_w, gate_bias)
        h = jnp.einsum('th,ehi->tei', x2d, w1_experts)
        a = relu2(h) * route_w[:, :, None].astype(x2d.dtype)
        routed = jnp.einsum('tei,eih->th', a, w2_experts)
        return (shared + routed).reshape(orig_shape)
    x = L0_attn_x
    xn = _layernorm(x, axis=-1)
    x = x + _L0_attn_ref(xn, L0_attn_norm_w, L0_attn_norm_b, L0_attn_x_proj_w, L0_attn_dt_proj_w, L0_attn_dt_proj_b, L0_attn_A_log, L0_attn_D_param, L0_attn_out_proj_w) + _L0_ffn_ref(xn, L0_ffn_gate_w, L0_ffn_gate_bias, L0_ffn_w_up_shared, L0_ffn_w_down_shared, L0_ffn_w1_experts, L0_ffn_w2_experts)
    return x

_drawn_inputs = setup_inputs


def setup_inputs(seed=0):
    import zlib

    import numpy as np

    out = dict(_drawn_inputs(seed))
    spreads = {'L0_attn_norm_w': (1.0, 0.2), 'L0_attn_norm_b': (0.0, 0.1), 'L0_attn_D_param': (1.0, 0.6)}
    factors = {'L0_attn_dt_proj_b': 8.0}
    for name, (base, spread) in spreads.items():
        noise = np.random.default_rng([zlib.crc32(name.encode()), seed]).standard_normal(out[name].shape)
        drawn = base * np.exp(spread * noise) if base else spread * noise
        out[name] = jnp.asarray(drawn.astype(out[name].dtype))
    for name, factor in factors.items():
        out[name] = (out[name] * factor).astype(out[name].dtype)
    return out
```

```python
import numpy as np
import concourse.bass as bass
from concourse import mybir
from contextlib import ExitStack

P = 128
T = 2048
NBATCH = 2
L = T // NBATCH
D = 256
N = 64
RANK = 128
PERIOD = 64
EXPERTS, TOPK, GROUPS, TOPG = 64, 6, 8, 4
INTER, SHARED = 128, 512
SCALE = 2.5
EPS = 1e-5
BIG = 1e30

TT = T // P
BLK = 8
CH = D // BLK
PAIRS = CH // 2
SL = NBATCH * PAIRS
GRP = 8
NFILL = 4
MOE_SLOTS = [s for s in range(SL) if s % 4 != 3]
MPI = len(MOE_SLOTS)
NMT = MPI * (BLK - 1)
NXT = NMT + 1
assert NMT >= (T * TOPK + EXPERTS * (P - 1)) // P
PARTS = 3
PLOAD = 16 * (2 * PARTS + 1)
RING = 12


def state_space_and_experts(nc, x, xprojT, dtT, vecs, A_l, outT, gateT, gbias, w_up, w_down, w1, w2, out):
    f32, bf16 = mybir.dt.float32, mybir.dt.bfloat16
    i32, u32 = mybir.dt.int32, mybir.dt.uint32
    ALU, ACT, AX = mybir.AluOpType, mybir.ActivationFunctionType, mybir.AxisListType

    ctx = ExitStack()
    with ctx:
        def sb(name, shape, dt=f32):
            return ctx.enter_context(nc.sbuf_tensor(name, shape, dt))

        def sem(name):
            return ctx.enter_context(nc.semaphore(name))

        parts_d = nc.dram_tensor("parts_d", (2, PARTS, D + CH, T), bf16, kind="Internal").ap()
        xg_d = nc.dram_tensor("xg_d", (NXT * P, D), f32, kind="Internal").ap()
        yg_d = nc.dram_tensor("yg_d", (NMT * P, D), f32, kind="Internal").ap()
        ys_d = nc.dram_tensor("ys_d", (D, NBATCH, L), f32, kind="Internal").ap()
        map_d = nc.dram_tensor("map_d", (2 * P, 1), u32, kind="Internal").ap()

        X = sb("X", [P, TT, D])
        XN = sb("XN", [P, TT, D])
        xnT = sb("xnT", [P, 2, T])
        vec = sb("vec", [P, 2, 4])
        wn = sb("wn", [P, TT, TOPK])
        slot = sb("slot", [P, TOPK, TT], i32)
        emap = sb("emap", [1, 2 * P], u32)
        ident = sb("ident", [P, P])
        Aneg = sb("Aneg", [P, P + PAIRS])
        Acur = sb("Acur", [P, NBATCH, PAIRS])
        B2 = sb("B2", [P, T])
        CB = sb("CB", [P, NBATCH, PERIOD, 32])
        H = sb("H", [P, 2 * GRP, L])
        U = sb("U", [P, 4, L])
        GS = sb("GS", [P, 2, L])
        PD = sb("PD", [PARTS * CH, NBATCH, L], bf16)
        PG = sb("PG", [PARTS * CH, NBATCH, L], bf16)
        sel = sb("sel", [PARTS * CH, PAIRS, P], bf16)
        YS = sb("YS", [P, 2, 512])
        XG = sb("XG", [P, 2, D])
        W1 = sb("W1", [P, 2, 2, INTER])
        W2 = sb("W2", [P, 2, D])
        XT = sb("XT", [P, 2, P])
        RL = sb("RL", [P, P])
        AS = sb("AS", [P, P])
        YO = sb("YO", [P, 2, D])
        ps = ctx.enter_context(nc.psum_tensor("ps", [P, 8, 512], f32))

        xn2T = H[:, 0:4, :].rearrange("p (h b) t -> p h (b t)", h=2)
        dpre = H[:, 4:6, :].rearrange("p b t -> p (b t)")
        Wproj = H[:, 6, 0:768].rearrange("p (k m) -> p k m", k=2)
        Wdt = H[:, 6, 768:1024]
        Wgate = U[:, 3, 0:128].rearrange("p (k m) -> p k m", k=2)
        z_t = H[:, 7, :]
        e_t = H[:, 8, :]
        l_t = H[:, 9, :]
        u_t = H[:, 10, :]
        dtg = H[:, 11:13, :]
        res = H[:, 13:15, :]
        prt = H[:, 15, :].bitcast(bf16).rearrange("p (a t) -> p a t", a=2)
        XN2 = H[:, 8:12, :].rearrange("p a (b c) -> p (a b) c", c=D)
        prt3 = GS[:, :, :].rearrange("p a t -> p (a t)").bitcast(bf16).rearrange("p (a t) -> p a t", a=4)
        wup = U[:, 2, :].rearrange("p (k m) -> p k m", k=2)
        wdn = U[:, 3, :].rearrange("p (k m) -> p k m", k=4)
        wo = GS[:, 0, 0:512].rearrange("p (k m) -> p k m", k=2)
        sc = H[:, 0, :]
        scb = H[:, 1, :]
        ra = H[:, 2, :]
        rb = H[:, 3, :]
        OH = H[:, 4:10, :]
        msel = H[:, 10, :]
        pos = H[:, 11, :]
        tot = H[:, 12, :]
        rc = H[:, 13, :]
        tri = H[:, 14, 0:64]
        iota_e = H[:, 14, 64:128]
        bias_b = H[:, 14, 128:192]
        small = H[:, 14, 192:1024]
        mbf = H[:, 15, 0:512].bitcast(bf16)
        ltri = H[:, 15, 512:576].bitcast(bf16)
        onesb = H[:, 15, 576:640].bitcast(bf16)

        st6 = sb("st6", [P, TT, 6])
        mv = sb("mv", [P, TT, 2])
        rstd = sb("rstd", [P, TT])
        rtmp = sb("rtmp", [P, 2, TT])

        x_in = sem("x_in")
        w_in = sem("w_in")
        w2_in = sem("w2_in")
        alog_in = sem("alog_in")
        wend_in = sem("wend_in")
        zeros_stored = sem("zeros_stored")
        zero_set = sem("zero_set")
        consts = sem("consts")
        gate_exp = sem("gate_exp")
        stats_ready = sem("stats_ready")
        sqrt_ready = sem("sqrt_ready")
        xn_ready = sem("xn_ready")
        job_done = sem("job_done")
        xnT_evac = sem("xnT_evac")
        xn2T_evac = sem("xn2T_evac")
        logits_mm = sem("logits_mm")
        act_evac = sem("act_evac")
        dve_evac = sem("dve_evac")
        proj_mm = sem("proj_mm")
        a_exp = sem("a_exp")
        z_ready = sem("z_ready")
        e_ready = sem("e_ready")
        l_ready = sem("l_ready")
        dt_ready_p = sem("dt_ready_p")
        part1_ready = sem("part1_ready")
        part2_ready = sem("part2_ready")
        split_ready = sem("split_ready")
        parts_stored = sem("parts_stored")
        oh_ready = sem("oh_ready")
        prefix_mm = sem("prefix_mm")
        map_ready = sem("map_ready")
        map_stored = sem("map_stored")
        map_loaded = sem("map_loaded")
        slots_ready = sem("slots_ready")
        scattered = sem("scattered")
        chain = sem("chain")
        pchain = sem("pchain")
        aneg_ready = sem("aneg_ready")
        dt_bcast = sem("dt_bcast")
        g_bcast = sem("g_bcast")
        a_ready = sem("a_ready")
        g_dve = sem("g_dve")
        g_act = sem("g_act")
        gs_ready = sem("gs_ready")
        u_pool = sem("u_pool")
        scan_done = sem("scan_done")
        y_filled = sem("y_filled")
        y_evac = sem("y_evac")
        moe_T = sem("moe_T")
        moe_xT = sem("moe_xT")
        moe_L1 = sem("moe_L1")
        moe_relu = sem("moe_relu")
        moe_sq = sem("moe_sq")
        moe_L2 = sem("moe_L2")
        moe_out = sem("moe_out")
        gathered = sem("gathered")
        z2_ready = sem("z2_ready")
        up_mm = sem("up_mm")
        up_relu = sem("up_relu")
        up_sq = sem("up_sq")
        fin_mm = sem("fin_mm")
        fin_free = sem("fin_free")
        comb = sem("comb")
        out_ready = sem("out_ready")
        out_stored = sem("out_stored")
        s_parts = [sem(f"parts_loaded{b}") for b in range(2)]
        s_ys = [sem(f"y_stored{b}") for b in range(2)]
        s_mx = [sem(f"moe_loaded{b}") for b in range(2)]
        s_mo = [sem(f"moe_stored{b}") for b in range(2)]
        s_yT = sem("yT_loaded")
        s_g = [sem(f"rows_gathered{b}") for b in range(RING)]
        s_os = [sem(f"out_stored{b}") for b in range(2)]

        def row(n):
            return H[:, 8 + (n % RING) // 4, (n % 4) * D:(n % 4 + 1) * D]

        def at_least_0(value):
            return max(value, 0) if isinstance(value, int) else value

        block = ctx.enter_context(nc.Block())

        JOBS = ([("xnT", q, "act") for q in range(8)] + [("xn2T", q, "dve") for q in range(8)]
                + [("logit", q, "act") for q in range(2)] + [("B", q, "dve") for q in range(4)]
                + [("dpre", q, "act") for q in range(4)] + [("dt", q, "dve") for q in range(8)]
                + [("C", q, "dve") for q in range(2)]
                + [("prefix", q, "dve") for q in range(4)])
        JN = {(k, q): n for n, (k, q, _) in enumerate(JOBS)}

        STORED = [0, 6, 12, 24]

        def evac_no(n):
            return sum(1 for _, _, c in JOBS[:n + 1] if c == JOBS[n][2])

        @block.sync
        def _(sp):
            xv = x.rearrange("(k p) d -> p k d", p=P)
            for c in range(4):
                sp.dma_start(X[:, 4 * c:4 * c + 4, :], xv[:, 4 * c:4 * c + 4, :]).then_inc(x_in, 16)
            sp.dma_start(vec[:, :, :], vecs).then_inc(w_in, 16)
            sp.dma_start(Wgate, gateT).then_inc(w_in, 16)
            sp.dma_start(Wproj, xprojT).then_inc(w_in, 16)
            sp.dma_start(Wdt, dtT).then_inc(w_in, 16)
            sp.dma_start(Aneg[:, 0:P], A_l).then_inc(w_in, 16)
            sp.wait_ge(zero_set, 1)
            zr = xg_d.rearrange("(a p) d -> p a d", p=P)
            for c in range(0, NXT, 8):
                n = min(8, NXT - c)
                sp.dma_start(zr[:, c:c + n, :], CB[:, :, :, :].rearrange("p b r m -> p (b r m)")[:, 0:n * D].rearrange("p (a d) -> p a d", d=D))\
                    .then_inc(zeros_stored, 16)
            for q in range(4):
                h, b = q // 2, q % 2
                for kind in range(2):
                    sp.wait_ge(split_ready, 2 * q + kind + 1)
                    for a in range(PARTS):
                        src = (prt[:, kind, :] if a == 2 else prt3[:, 2 * kind + a, :])
                        sp.dma_start(parts_d[kind, a, h * P:(h + 1) * P, b * L:(b + 1) * L], src)\
                            .then_inc(parts_stored, 16)
                        if h == 1:
                            sp.dma_start(parts_d[kind, a, D:D + CH, b * L:(b + 1) * L], src[0:CH, :])\
                                .then_inc(parts_stored, 16)
            sp.wait_ge(parts_stored, 16 * (24 + 12))

            def load_parts(block_no, b):
                sp.dma_start(Acur[:, b, :], Aneg[:, bass.ds(block_no * PAIRS, PAIRS)]).then_inc(s_parts[b], 16)
                for kind, dst in ((0, PD), (1, PG)):
                    for a in range(PARTS):
                        sp.dma_start(dst[a * CH:(a + 1) * CH, b, :],
                                     parts_d[kind, a, bass.ds(block_no * CH, CH), b * L:(b + 1) * L])\
                            .then_inc(s_parts[b], 16)

            sp.wait_ge(aneg_ready, 2)
            load_parts(0, 0)
            sp.dma_start(bias_b, gbias.partition_broadcast(P)).then_inc(w2_in, 16)
            sp.wait_ge(map_ready, 1)
            for c in range(2):
                sp.dma_start(map_d[c * P:(c + 1) * P, :],
                             small[:, 820 + c:821 + c].bitcast(u32)).then_inc(map_stored, 16)
            sp.wait_ge(map_stored, 32)
            sp.dma_start(emap[:, :], map_d.rearrange("a b -> b a")).then_inc(map_loaded, 16)
            sp.wait_ge(map_loaded, 16)

            def load_expert(m, par):
                e = sp.value_load(emap[0:1, bass.ds(m, 1)], min_val=0, max_val=EXPERTS - 1)
                sp.dma_start(XG[:, par, :], xg_d[bass.ds(m * P, P), :]).then_inc(s_mx[par], 16)
                sp.dma_start(W1[:, par, :, :],
                             w1[bass.ds(e, 1)].rearrange("e (k p) i -> p (e k) i", p=P)).then_inc(s_mx[par], 16)
                sp.dma_start(W2[:, par, :],
                             w2[bass.ds(e, 1)].rearrange("e p n -> (e p) n")).then_inc(s_mx[par], 16)

            def store_fill(F, blk, s, f):
                G = F // NFILL if isinstance(F, int) else None
                par = f % 2
                sp.wait_ge(y_evac, F + 1)
                b, half = (s // PAIRS), (s // GRP) % 2
                for d2 in range(2):
                    dst = ys_d.rearrange("(k w g q) b (f j x) -> k w b f q j g x", k=BLK, w=2, q=2, f=NFILL, j=4)
                    dst = dst[bass.ds(blk, 1), half, b, f, d2].rearrange("k j g x -> (k j) g x")
                    src = YS[d2:96 + d2 + 1:32, par, :].rearrange("j (g x) -> j g x", g=GRP)
                    sp.dma_start(dst, src).then_inc(s_ys[par], 16)

            def body(it, moe):
                sp.wait_ge(g_bcast, it * SL)
                sp.wait_ge(a_ready, it * SL)
                load_parts(it, 1)
                for s in range(SL):
                    if s == PAIRS:
                        sp.wait_ge(g_bcast, it * SL + PAIRS)
                        sp.wait_ge(a_ready, it * SL + PAIRS)
                        load_parts(it + 1, 0)
                    if s in MOE_SLOTS and moe:
                        j = MOE_SLOTS.index(s)
                        m = (it - 1) * MPI + j
                        sp.wait_ge(moe_L2, m)
                        load_expert(m + 1, (j + 1) % 2)
                    if s % 2 == 1:
                        f = (s % GRP) // 2
                        F = (it * 4 + s // GRP - 1) * NFILL + f
                        if not (isinstance(F, int) and F < 0):
                            ps_, pblk = ((s - GRP), it) if s >= GRP else (s - GRP + SL, it - 1)
                            store_fill(F, pblk, ps_, f)
                    if s in MOE_SLOTS and moe:
                        sp.wait_ge(moe_out, m + 1)
                        sp.dma_start(yg_d[bass.ds(m * P, P), :], YO[:, j % 2, :]).then_inc(s_mo[j % 2], 16)

            body(0, False)
            sp.wait_ge(scattered, 16 * TT * TOPK)
            load_expert(0, 0)
            with sp.Fori(1, BLK) as it:
                body(it, True)
            for f in range(NFILL):
                store_fill((BLK * 4 - 1) * NFILL + f, BLK - 1, SL - GRP, f)
            sp.wait_ge(scan_done, BLK * SL)
            sp.dma_start(wup, w_up.rearrange("(k p) m -> p k m", p=P)).then_inc(wend_in, 16)
            sp.dma_start(wdn, w_down.rearrange("(k p) m -> p k m", p=P)).then_inc(wend_in, 16)
            sp.dma_start(wo, outT).then_inc(wend_in, 16)
            for par in range(2):
                sp.wait_ge(s_ys[par], 2 * 16 * (BLK * 4 * NFILL // 2))
            for h in range(2):
                sp.dma_start(H[:, 4 + 2 * h:6 + 2 * h, :],
                             ys_d[h * P:(h + 1) * P, :, :]).then_inc(s_yT, 16)
            for k in range(TT):
                sp.wait_ge(out_ready, k + 1)
                sp.dma_start(out[k * P:(k + 1) * P, :], YO[:, k % 2, :]).then_inc(s_os[k % 2], 16)
            for par in range(2):
                sp.wait_ge(s_os[par], 16 * TT // 2)
                sp.wait_ge(s_mo[par], 16 * NMT // 2)
                sp.wait_ge(s_mx[par], at_least_0(48 * (NMT // 2 + (1 - par))))
            sp.wait_ge(s_parts[0], PLOAD * (BLK + 1))

        @block.gpsimd
        def _(pool):
            nc.gpsimd.memset(CB[:, :, :, :], 0.0).then_inc(zero_set, 1)
            nc.gpsimd.memset(ident[:, :], 0.0).then_inc(pchain, 1)
            nc.gpsimd.memset(sel[:, :, :], 0.0).then_inc(pchain, 1)
            pool.wait_ge(pchain, 1)
            nc.gpsimd.affine_select(out=ident[:, :], in_=ident[:, :], compare_op=ALU.not_equal, fill=1.0,
                                    base=0, pattern=[[-1, P]], channel_multiplier=1).then_inc(consts, 1)
            pool.wait_ge(pchain, 2)
            for a in range(PARTS):
                pool.wait_ge(consts, a + 1)
                v = sel[a * CH:(a + 1) * CH, :, :].rearrange("p j (h n) -> p j h n", h=2)
                nc.gpsimd.affine_select(out=v, in_=v, compare_op=ALU.not_equal, fill=1.0, base=0,
                                        pattern=[[-2, PAIRS], [-1, 2], [0, N]], channel_multiplier=1)\
                    .then_inc(consts, 1)
            pool.wait_ge(consts, 4)
            pool.wait_ge(parts_stored, 16 * (24 + 12))
            pool.wait_ge(dt_ready_p, 8)
            nc.gpsimd.memset(tri, 1.0).then_inc(pchain, 1)
            nc.gpsimd.memset(ltri, 1.0).then_inc(pchain, 1)
            nc.gpsimd.memset(onesb, 1.0).then_inc(consts, 1)
            nc.gpsimd.memset(U[:, 0, 0:1], 0.0).then_inc(u_pool, 2)
            nc.gpsimd.iota(iota_e, pattern=[[1, EXPERTS]], base=0, channel_multiplier=0,
                           allow_small_or_imprecise_dtypes=True).then_inc(consts, 1)
            nc.gpsimd.iota(small[:, 800:802], pattern=[[P, 2]], base=0, channel_multiplier=1,
                           allow_small_or_imprecise_dtypes=True).then_inc(consts, 1)
            pool.wait_ge(pchain, 4)
            tv = tri.rearrange("p (g h) -> p g h", g=GROUPS)
            nc.gpsimd.affine_select(out=tv, in_=tv, compare_op=ALU.is_gt, fill=0.0, base=0,
                                    pattern=[[1, GROUPS], [-1, GROUPS]], channel_multiplier=0)\
                .then_inc(consts, 1)
            nc.gpsimd.affine_select(out=ltri, in_=ltri, compare_op=ALU.is_gt, fill=0.0, base=0,
                                    pattern=[[1, P]], channel_multiplier=-1).then_inc(consts, 1)

            def scatter(k, t):
                pool.indirect_dma_start(xg_d, bass.IndirectOffsetOnAxis(ap=slot[:, k, t:t + 1].bitcast(u32), axis=0),
                                        XN[:, t, :], None).then_inc(scattered, 16)

            def body(it, moe):
                for s in range(SL):
                    i = it * SL + s
                    if not moe:
                        for q in range(3):
                            scatter((3 * s + q) // TT, (3 * s + q) % TT)
                    elif s % 2 == 0:
                        v = (it - 1) * (SL // 2) + s // 2
                        pool.wait_ge(gs_ready, v + 1)
                        pool.wait_ge(scan_done, at_least_0(i - 3))
                        nc.gpsimd.tensor_tensor(U[:, s % 4, :], GS[:, (s // 2) % 2, :],
                                                B2[:, (s // PAIRS) * L:(s // PAIRS + 1) * L], ALU.mult)\
                            .then_inc(u_pool, 1)

            pool.wait_ge(slots_ready, 1)
            pool.wait_ge(zeros_stored, 16 * ((NXT + 7) // 8))
            body(0, False)
            with pool.Fori(1, BLK) as it:
                body(it, True)
            for par in range(2):
                pool.wait_ge(s_mo[par], 16 * NMT // 2)
            pool.wait_ge(y_filled, BLK * 4 * NFILL)
            for t in range(TT):
                for k in range(TOPK):
                    n = t * TOPK + k
                    pool.wait_ge(comb, at_least_0(n - RING + 1))
                    pool.indirect_dma_start(row(n), None, yg_d,
                                            bass.IndirectOffsetOnAxis(ap=slot[:, k, t:t + 1].bitcast(u32), axis=0))\
                        .then_inc(s_g[n % RING], 16)

        @block.scalar
        def _(act):
            for ln in range(2):
                act.wait_ge(stats_ready, ln + 1)
                nc.scalar.activation(rstd[:, :], rtmp[:, 0, :], ACT.Sqrt).then_inc(sqrt_ready, 1)
            for q in range(8):
                act.wait_ge(job_done, JN["xnT", q] + 1)
                h, g4 = q % 2, q // 2
                nc.scalar.copy(xnT[:, h, 512 * g4:512 * g4 + 512], ps[:, JN["xnT", q] % 8, :])\
                    .then_inc(act_evac, 1)
            for q in range(2):
                n = JN["logit", q]
                act.wait_ge(job_done, n + 1)
                nc.scalar.activation(U[:, 2, q * 512:(q + 1) * 512], ps[:, n % 8, :], ACT.Exp, scale=-1.0)\
                    .then_inc(act_evac, 1)
            act.wait_ge(w_in, 80)
            nc.scalar.activation(Aneg[:, 0:P], Aneg[:, 0:P], ACT.Exp).then_inc(a_exp, 1)
            for q in range(4):
                n = JN["dpre", q]
                act.wait_ge(job_done, n + 1)
                nc.scalar.copy(dpre[:, 512 * q:512 * q + 512], ps[:, n % 8, :]).then_inc(act_evac, 1)
            for q in range(4):
                act.wait_ge(z_ready, q + 1)
                nc.scalar.activation(e_t, e_t, ACT.Exp).then_inc(e_ready, 1)
                act.wait_ge(e_ready, 2 * q + 1)
                nc.scalar.activation(l_t, e_t, ACT.Ln, bias=1.0).then_inc(e_ready, 1)
                for kind in range(2):
                    act.wait_ge(dt_ready_p, 2 * q + kind + 1)
                    act.wait_ge(parts_stored, 16 * STORED[q])
                    nc.scalar.copy(prt3[:, 2 * kind, :], dtg[:, kind, :]).then_inc(part1_ready, 1)
                for kind in range(2):
                    act.wait_ge(part2_ready, 2 * q + kind + 1)
                    nc.scalar.copy(prt3[:, 2 * kind + 1, :], res[:, kind, :]).then_inc(part1_ready, 1)

            act.wait_ge(parts_stored, 16 * (24 + 12))

            def body(it, moe):
                for s in range(SL):
                    i = it * SL + s
                    b, pair = s // PAIRS, s % PAIRS
                    if pair == 0:
                        act.wait_ge(s_parts[b], (it + 1) * PLOAD)
                    act.wait_ge(dt_bcast, i + 1)
                    dtp = ps[:, 2 * (s % 2):2 * (s % 2) + 2, :]
                    nc.scalar.activation(dtp, dtp, ACT.Exp, scale=Acur[:, b, pair:pair + 1])\
                        .then_inc(a_ready, 1)
                    if moe and s % 2 == 0:
                        v = (it - 1) * (SL // 2) + s // 2
                        act.wait_ge(g_bcast, i + 1)
                        act.wait_ge(u_pool, v + 1)
                        nc.scalar.copy(GS[:, (s // 2) % 2, :].rearrange("p (a c) -> p a c", a=2), ps[:, 4:6, :])\
                            .then_inc(gs_ready, 1)
                    if moe and s in MOE_SLOTS:
                        m = (it - 1) * MPI + MOE_SLOTS.index(s)
                        act.wait_ge(moe_T, m + 1)
                        nc.scalar.copy(XT[:, :, :].rearrange("p k t -> p (k t)"), ps[:, 7, 0:D])\
                            .then_inc(moe_xT, 1)
                        act.wait_ge(moe_relu, m + 1)
                        act.wait_ge(moe_L2, m)
                        nc.scalar.activation(AS[:, :], RL[:, :], ACT.Square).then_inc(moe_sq, 1)
                    if s % 2 == 1:
                        f = (s % GRP) // 2
                        evac_fill((it * 4 + s // GRP - 1) * NFILL + f, f)

            def evac_fill(F, f):
                if isinstance(F, int) and F < 0:
                    return
                act.wait_ge(y_filled, F + 1)
                act.wait_ge(s_ys[f % 2], at_least_0(32 * (F // 2) if isinstance(F, int) else (F - f % 2) * 16))
                nc.scalar.copy(YS[:, f % 2, :], ps[:, 6, :]).then_inc(y_evac, 1)

            body(0, False)
            with act.Fori(1, BLK) as it:
                body(it, True)
            for f in range(NFILL):
                evac_fill((BLK * 4 - 1) * NFILL + f, f)
            for q in range(4):
                for it_ in range(4):
                    n = 4 * q + it_
                    act.wait_ge(up_mm, n + 1)
                    act.wait_ge(up_sq, at_least_0(n - 1))
                    nc.scalar.activation(U[:, n % 2, 0:512], ps[:, n % 2, :], ACT.Relu).then_inc(up_relu, 1)

        @block.vector
        def _(dve):
            count = [0]

            def link(ins):
                count[0] += 1
                ins.then_inc(chain, 1)
                dve.wait_ge(chain, count[0])

            V = nc.vector

            def layernorm(src, dst, ln):
                for k in range(TT):
                    if ln == 0 and k == 0:
                        dve.wait_ge(x_in, 64)
                    ins = V.bn_stats(st6[:, k, :], src[:, k, :])
                    if k == TT - 1:
                        link(ins)
                for k in range(TT):
                    ins = V.bn_aggr(mv[:, k, :], st6[:, k, :])
                link(ins)
                V.tensor_scalar(rtmp[:, 0, :], mv[:, :, 1], EPS, None, ALU.add).then_inc(stats_ready, 1)
                dve.wait_ge(sqrt_ready, ln + 1)
                link(V.reciprocal(rstd[:, :], rstd[:, :]))
                link(V.tensor_tensor(rtmp[:, 1, :], rstd[:, :], rstd[:, :], ALU.mult))
                link(V.tensor_tensor(rtmp[:, 1, :], rtmp[:, 1, :], rtmp[:, 0, :], ALU.mult))
                link(V.tensor_scalar(rtmp[:, 1, :], rtmp[:, 1, :], -0.5, 1.5, ALU.mult, ALU.add))
                link(V.tensor_tensor(rstd[:, :], rstd[:, :], rtmp[:, 1, :], ALU.mult))
                for k in range(TT):
                    ins = V.tensor_scalar(dst[:, k, :], src[:, k, :], mv[:, k, 0:1], rstd[:, k:k + 1],
                                          ALU.subtract, ALU.mult)
                ins.then_inc(xn_ready, 1)
                dve.wait_ge(xn_ready, ln + 1)

            layernorm(X, XN, 0)
            layernorm(XN, XN2, 1)
            dve.wait_ge(w_in, 80)
            for q in range(8):
                n = JN["xn2T", q]
                dve.wait_ge(job_done, n + 1)
                h, g4 = q % 2, q // 2
                V.tensor_scalar(xn2T[:, h, 512 * g4:512 * g4 + 512], ps[:, n % 8, :], vec[:, h, 0:1], vec[:, h, 1:2],
                                ALU.mult, ALU.add).then_inc(dve_evac, 1)
            for q in range(4):
                n = JN["B", q]
                dve.wait_ge(job_done, n + 1)
                V.tensor_copy(B2[:, 512 * q:512 * q + 512], ps[:, n % 8, :]).then_inc(dve_evac, 1)
            dve.wait_ge(a_exp, 1)
            V.tensor_scalar(Aneg[:, 0:P], Aneg[:, 0:P], -1.0, None, ALU.mult).then_inc(aneg_ready, 1)
            V.memset(Aneg[:, P:], 0.0).then_inc(aneg_ready, 1)

            for q in range(4):
                h, b = q // 2, q % 2
                for c in range(2):
                    n = JN["dt", 2 * q + c]
                    dve.wait_ge(job_done, n + 1)
                    ins = V.tensor_scalar(z_t[:, 512 * c:512 * c + 512], ps[:, n % 8, :], vec[:, h, 2:3], None, ALU.add)
                    ins.then_inc(dve_evac, 1)
                dve.wait_ge(dve_evac, evac_no(n))
                V.scalar_tensor_tensor(e_t, z_t, -1.0, z_t, ALU.mult, ALU.min).then_inc(z_ready, 1)
                dve.wait_ge(e_ready, 2 * q + 2)
                link(V.tensor_scalar(u_t, e_t, 1.0, None, ALU.add))
                link(V.scalar_tensor_tensor(u_t, u_t, -1.0, e_t, ALU.add, ALU.subtract))
                link(V.tensor_tensor(l_t, l_t, u_t, ALU.subtract))
                V.scalar_tensor_tensor(dtg[:, 0, :], z_t, 0.0, l_t, ALU.max, ALU.add).then_inc(dt_ready_p, 1)
                dve.wait_ge(dt_ready_p, 2 * q + 1)
                V.tensor_tensor(dtg[:, 1, :], dtg[:, 0, :], xn2T[:, h, b * L:(b + 1) * L], ALU.mult)\
                    .then_inc(dt_ready_p, 1)
                for kind in range(2):
                    dve.wait_ge(part1_ready, 4 * q + kind + 1)
                    dve.wait_ge(dt_ready_p, 2 * q + kind + 1)
                    V.tensor_tensor(res[:, kind, :], dtg[:, kind, :], prt3[:, 2 * kind, :], ALU.subtract)\
                        .then_inc(part2_ready, 1)
                for kind in range(2):
                    dve.wait_ge(part1_ready, 4 * q + 2 + kind + 1)
                    dve.wait_ge(parts_stored, 16 * STORED[q])
                    V.tensor_tensor(prt[:, kind, :], res[:, kind, :], prt3[:, 2 * kind + 1, :], ALU.subtract)\
                        .then_inc(split_ready, 1)

            dve.wait_ge(zeros_stored, 16 * ((NXT + 7) // 8))
            for b in range(2):
                n = JN["C", b]
                dve.wait_ge(job_done, n + 1)
                V.tensor_copy(CB[0:N, b, :, 0], ps[0:N, n % 8, 0:PERIOD])
                V.tensor_copy(CB[N:P, b, :, 1], ps[N:P, n % 8, 0:PERIOD]).then_inc(dve_evac, 1)

            dve.wait_ge(split_ready, 8)
            dve.wait_ge(act_evac, evac_no(JN["dpre", 3]))
            dve.wait_ge(w2_in, 16)
            dve.wait_ge(consts, 9)
            dve.wait_ge(parts_stored, 16 * 36)
            t8 = lambda a: a.rearrange("p (g e) -> p g e", e=8)
            t64 = lambda a: a.rearrange("p (t e) -> p t e", e=EXPERTS)
            g1, g2, g3, gs, pen = (small[:, 128 * n:128 * n + 128] for n in range(5))
            link(V.tensor_scalar(sc, U[:, 2, :], 1.0, None, ALU.add))
            link(V.reciprocal(sc, sc))
            link(V.tensor_tensor(t64(scb), t64(sc), bias_b.unsqueeze(1).broadcast_to((P, TT, EXPERTS)), ALU.add))
            bc8 = lambda a: a.unsqueeze(2).broadcast_to((P, P, 8))
            link(V.tensor_reduce(g1, t8(scb), AX.X, ALU.max))
            link(V.tensor_tensor(t8(ra), t8(scb), bc8(g1), ALU.is_equal))
            V.tensor_reduce(g2, t8(ra), AX.X, ALU.add)
            link(V.scalar_tensor_tensor(rb, ra, -BIG, scb, ALU.mult, ALU.add))
            V.tensor_reduce(g3, t8(rb), AX.X, ALU.max)
            link(V.tensor_scalar(g2, g2, 1.5, -BIG, ALU.is_lt, ALU.mult))
            link(V.tensor_tensor(g2, g2, g1, ALU.add))
            link(V.tensor_tensor(g3, g3, g2, ALU.max))
            link(V.tensor_tensor(gs, g1, g3, ALU.add))
            v3 = lambda a: a.rearrange("p (t g h) -> p t g h", g=GROUPS, h=GROUPS)
            gsv = gs.rearrange("p (t g) -> p t g", g=GROUPS)
            gh = gsv.unsqueeze(2).broadcast_to((P, TT, GROUPS, GROUPS))
            gg = gsv.unsqueeze(3).broadcast_to((P, TT, GROUPS, GROUPS))
            link(V.tensor_tensor(v3(rb), gh, gg, ALU.is_equal))
            link(V.tensor_tensor(t64(rb), t64(rb), tri.unsqueeze(1).broadcast_to((P, TT, 64)), ALU.mult))
            link(V.tensor_tensor(v3(ra), gh, gg, ALU.is_gt))
            link(V.tensor_tensor(ra, ra, rb, ALU.add))
            link(V.tensor_reduce(g2, t8(ra), AX.X, ALU.add))
            link(V.tensor_scalar(pen, g2, TOPG - 0.5, BIG, ALU.is_lt, ALU.mult))
            link(V.tensor_scalar(pen, pen, -BIG, None, ALU.add))
            link(V.tensor_tensor(t8(scb), t8(scb), bc8(pen), ALU.add))
            top = g1.rearrange("p (t e) -> p t e", e=8)
            idx = g2.bitcast(u32).rearrange("p (t e) -> p t e", e=8)
            idf = g3.rearrange("p (t e) -> p t e", e=8)
            for t in range(TT):
                ins = V.max(top[:, t, :], t64(scb)[:, t, :])
            link(ins)
            for t in range(TT):
                ins = V.max_index(idx[:, t, :], top[:, t, :], t64(scb)[:, t, :])
            link(ins)
            link(V.tensor_copy(idf, idx))
            iob = iota_e.unsqueeze(1).broadcast_to((P, TT, EXPERTS))
            for k in range(TOPK):
                link(V.tensor_tensor(t64(OH[:, k, :]), iob, idf[:, :, k:k + 1].broadcast_to((P, TT, EXPERTS)),
                                     ALU.is_equal))
                link(V.tensor_tensor(ra, OH[:, k, :], sc, ALU.mult))
                link(V.tensor_reduce(wn[:, :, k], t64(ra), AX.X, ALU.add))
                if k == 1:
                    link(V.tensor_tensor(msel, OH[:, 0, :], OH[:, 1, :], ALU.add))
                elif k > 1:
                    link(V.tensor_tensor(msel, msel, OH[:, k, :], ALU.add))
            V.tensor_copy(mbf, msel).then_inc(oh_ready, 1)
            wsum = small[:, 640:656]
            link(V.tensor_reduce(wsum, wn[:, :, :], AX.X, ALU.add))
            link(V.tensor_scalar(wsum, wsum, 1e-20, None, ALU.add))
            link(V.reciprocal(wsum, wsum))
            link(V.tensor_scalar(wsum, wsum, SCALE, None, ALU.mult))
            link(V.tensor_tensor(wn[:, :, :], wn[:, :, :], wsum.unsqueeze(2).broadcast_to((P, TT, TOPK)), ALU.mult))
            for q in range(4):
                n = JN["prefix", q]
                dve.wait_ge(job_done, n + 1)
                dst = pos if q < 2 else tot
                V.tensor_copy(dst[:, 512 * (q % 2):512 * (q % 2) + 512], ps[:, n % 8, :]).then_inc(dve_evac, 1)
            dve.wait_ge(dve_evac, evac_no(JN["prefix", 3]))
            run = t64(rb)
            link(V.tensor_copy(run[:, 0, :], t64(tot)[:, 0, :]))
            for t in range(1, TT):
                link(V.tensor_tensor(run[:, t, :], run[:, t - 1, :], t64(tot)[:, t, :], ALU.add))
            link(V.tensor_tensor(t64(pos)[:, 1:, :], t64(pos)[:, 1:, :], run[:, :TT - 1, :], ALU.add))
            nt = rc[:, 0:64]
            nti = rc[:, 64:128].bitcast(i32)
            incl = rc[:, 128:192]
            one = rc[:, 192:256]
            V.memset(one, 1.0)
            link(V.tensor_scalar(nt, run[:, TT - 1, :], float(P - 1), None, ALU.add))
            link(V.tensor_copy(nti, nt))
            link(V.tensor_scalar(nti, nti, 7, None, ALU.logical_shift_right))
            link(V.tensor_copy(nt, nti))
            link(V.tensor_tensor_scan(incl, one, nt, 0.0, ALU.mult, ALU.add))
            link(V.tensor_tensor(nt, incl, nt, ALU.subtract))
            link(V.tensor_scalar(nt, nt, float(P), None, ALU.mult))
            link(V.tensor_tensor(t64(pos), t64(pos), nt.unsqueeze(1).broadcast_to((P, TT, EXPERTS)), ALU.add))
            for c in range(2):
                link(V.tensor_scalar(one, incl, small[:, 800 + c:801 + c], None, ALU.is_le))
                link(V.tensor_reduce(small[:, 810 + c:811 + c], one, AX.X, ALU.add))
            link(V.tensor_scalar(small[:, 810:812], small[:, 810:812], float(EXPERTS - 1), None, ALU.min))
            V.tensor_copy(small[:, 820:822].bitcast(u32), small[:, 810:812]).then_inc(map_ready, 1)
            for k in range(TOPK):
                link(V.tensor_tensor(ra, OH[:, k, :], pos, ALU.mult))
                link(V.tensor_reduce(rc[:, 256 + 16 * k:272 + 16 * k], t64(ra), AX.X, ALU.add))
            V.tensor_copy(slot[:, :, :], rc[:, 256:256 + 96].rearrange("p (k t) -> p k t", k=TOPK))\
                .then_inc(slots_ready, 1)
            dve.wait_ge(map_stored, 32)
            dve.wait_ge(slots_ready, 1)

            def product(i, s, u, on_dve):
                b = s // PAIRS
                dve.wait_ge(g_bcast, i + 1)
                V.tensor_tensor(U[:, s % 4, :].rearrange("p (a c) -> p a c", a=2), ps[:, 4:6, :],
                                B2[:, b * L:(b + 1) * L].rearrange("p (a c) -> p a c", a=2), ALU.mult)\
                    .then_inc(g_dve, 1)

            def body(it, moe):
                for s in range(SL):
                    i = it * SL + s
                    G = it * 4 + s // GRP
                    if not moe:
                        nd = i
                    else:
                        nd = SL + (it - 1) * (SL // 2) + s // 2
                    if not moe:
                        product(i, s, None, True)
                    if s % GRP == 0:
                        dve.wait_ge(y_filled, at_least_0((G - 1) * NFILL))
                    if moe and s % 2 == 0:
                        dve.wait_ge(u_pool, at_least_0((it - 1) * (SL // 2) + s // 2 + 3))
                    else:
                        dve.wait_ge(g_dve, nd + 1)
                    dve.wait_ge(a_ready, i + 1)
                    V.tensor_tensor_scan(H[:, (s // GRP % 2) * GRP + s % GRP, :],
                                         ps[:, 2 * (s % 2):2 * (s % 2) + 2, :].rearrange("p a c -> p (a c)"),
                                         U[:, s % 4, :], 0.0, ALU.mult, ALU.add).then_inc(scan_done, 1)
                    if moe and s in MOE_SLOTS:
                        j = MOE_SLOTS.index(s)
                        m = (it - 1) * MPI + j
                        dve.wait_ge(moe_L1, m + 1)
                        dve.wait_ge(moe_sq, m)
                        V.tensor_scalar(RL[:, :], ps[:, 7, 256:384], 0.0, None, ALU.max).then_inc(moe_relu, 1)
                    if moe and s % 2 == 0:
                        product(i + 1, s + 1, None, True)
                    if moe and s in MOE_SLOTS:
                        dve.wait_ge(moe_L2, m + 1)
                        dve.wait_ge(s_mo[j % 2], at_least_0((m - j % 2) * 8))
                        V.tensor_copy(YO[:, j % 2, :], ps[:, 7, 0:D]).then_inc(moe_out, 1)

            body(0, False)
            with dve.Fori(1, BLK) as it:
                body(it, True)

            dve.wait_ge(s_yT, 32)
            for h in range(2):
                for b in range(2):
                    yv = H[:, 4 + 2 * h + b, :].rearrange("p (r c) -> p r c", r=PERIOD)
                    xv = xnT[:, h, b * L:(b + 1) * L].rearrange("p (c r) -> p r c", r=PERIOD)
                    zv = H[:, 12 + 2 * h + b, :].rearrange("p (c r) -> p r c", r=PERIOD)
                    V.scalar_tensor_tensor(zv, xv, vec[:, h, 3:4], yv, ALU.mult, ALU.add).then_inc(z2_ready, 1)
            for q in range(4):
                for i4 in range(4):
                    n = 4 * q + i4
                    dve.wait_ge(up_relu, n + 1)
                    V.tensor_tensor(H[:, i4 // 2, (i4 % 2) * 512:(i4 % 2) * 512 + 512], U[:, n % 2, 0:512],
                                    U[:, n % 2, 0:512], ALU.mult).then_inc(up_sq, 1)
                for t in range(4 * q, 4 * q + 4):
                    for k in range(TOPK):
                        n = t * TOPK + k
                        dve.wait_ge(s_g[n % RING], 16 * (n // RING + 1))
                        if n:
                            dve.wait_ge(comb, n)
                        V.scalar_tensor_tensor(X[:, t, :], row(n), wn[:, t, k:k + 1], X[:, t, :], ALU.mult, ALU.add)\
                            .then_inc(comb, 1)
                    dve.wait_ge(comb, TOPK * (t + 1))
                    dve.wait_ge(fin_mm, t + 1)
                    if t < 2:
                        dve.wait_ge(s_mo[t % 2], 16 * NMT // 2)
                    else:
                        dve.wait_ge(s_os[t % 2], 16 * (t // 2))
                    V.tensor_tensor(YO[:, t % 2, :], ps[:, 2 + t % 2, 0:D], X[:, t, :], ALU.add)\
                        .then_inc(out_ready, 1)

        @block.tensor
        def _(pe):
            mm = nc.tensor.matmul
            for n, (kind, q, _) in enumerate(JOBS):
                bank = ps[:, n % 8, :]
                if n >= 8 and JOBS[n - 8][2] == "act":
                    pe.wait_ge(act_evac, evac_no(n - 8))
                elif n >= 8:
                    pe.wait_ge(dve_evac, evac_no(n - 8))
                if kind in ("xnT", "xn2T"):
                    if q == 0:
                        pe.wait_ge(consts, 1)
                        pe.wait_ge(xn_ready, 1 if kind == "xnT" else 2)
                    src = XN if kind == "xnT" else XN2
                    h, g4 = q % 2, q // 2
                    for j in range(4):
                        ins = nc.tensor.transpose(bank[:, j * P:(j + 1) * P], src[:, 4 * g4 + j, h * P:(h + 1) * P],
                                                  ident[:, :])
                elif kind == "logit":
                    if q == 0:
                        pe.wait_ge(w_in, 80)
                        pe.wait_ge(act_evac, 8)
                    for j in range(8):
                        t = 8 * q + j
                        for k in range(2):
                            ins = mm(bank[:, j * 64:(j + 1) * 64], xnT[:, k, t * P:(t + 1) * P], Wgate[:, k, :],
                                     start=(k == 0), stop=(k == 1))
                elif kind in ("B", "C", "dpre"):
                    if (kind, q) == ("B", 0):
                        pe.wait_ge(dve_evac, 8)
                    m0 = {"dpre": 0, "B": P, "C": 2 * P}[kind]
                    for k in range(2):
                        if kind == "C":
                            ins = mm(bank[:, 0:PERIOD], Wproj[:, k, m0:m0 + P], xn2T[:, k, q * L:q * L + PERIOD],
                                     start=(k == 0), stop=(k == 1))
                        else:
                            ins = mm(bank, Wproj[:, k, m0:m0 + P], xn2T[:, k, 512 * q:512 * q + 512],
                                     start=(k == 0), stop=(k == 1))
                elif kind == "dt":
                    if q == 0:
                        pe.wait_ge(act_evac, evac_no(JN["dpre", 3]))
                    h, tq = q // 4, q % 4
                    ins = mm(bank, Wdt[:, h * P:(h + 1) * P], dpre[:, 512 * tq:512 * tq + 512], start=True, stop=True)
                else:
                    if q == 0:
                        pe.wait_ge(oh_ready, 1)
                        pe.wait_ge(consts, 9)
                    ins = mm(bank, ltri if q < 2 else onesb, mbf[:, 512 * (q % 2):512 * (q % 2) + 512],
                             start=True, stop=True)
                ins.then_inc(job_done, 1)
            pe.wait_ge(dve_evac, evac_no(JN["prefix", 3]))
            pe.wait_ge(act_evac, evac_no(JN["dpre", 3]))

            def y_quarter(F, s, b, qq, last):
                f = F[1]
                hb = H[:, (s // GRP % 2) * GRP:(s // GRP % 2) * GRP + GRP, :]\
                    .rearrange("p g (c r) -> p g c r", r=PERIOD)
                for j in range(4):
                    r = f * 16 + j * 4 + qq
                    o = ps[32 * j:32 * j + 32, 6, :].rearrange("p (g a c) -> p g a c", g=GRP, a=4)[:, :, qq, :]
                    ins = mm(o, CB[:, b, r, :], hb[:, :, :, r], start=True, stop=True)
                if last:
                    ins.then_inc(y_filled, 1)

            def body(it, moe):
                for s in range(SL):
                    i = it * SL + s
                    b, pair = s // PAIRS, s % PAIRS
                    if pair == 0:
                        pe.wait_ge(s_parts[b], (it + 1) * PLOAD)
                    pe.wait_ge(scan_done, at_least_0(i - 1))
                    for c in range(2):
                        ins = mm(ps[:, 2 * (s % 2) + c, :], sel[:, pair, :], PD[:, b, 512 * c:512 * c + 512],
                                 start=True, stop=True)
                    ins.then_inc(dt_bcast, 1)
                    if not moe:
                        pe.wait_ge(g_dve, i)
                    elif s % 2 == 0:
                        pe.wait_ge(g_dve, at_least_0(SL + (it - 1) * (SL // 2) + s // 2))
                    else:
                        pe.wait_ge(gs_ready, at_least_0((it - 1) * (SL // 2) + s // 2 + 1))
                    for c in range(2):
                        ins = mm(ps[:, 4 + c, :], sel[:, pair, :], PG[:, b, 512 * c:512 * c + 512],
                                 start=True, stop=True)
                    ins.then_inc(g_bcast, 1)
                    isM = moe and s in MOE_SLOTS
                    if isM:
                        j = MOE_SLOTS.index(s)
                        m = (it - 1) * MPI + j
                        par = j % 2
                        pe.wait_ge(s_mx[par], at_least_0(((m - par) // 2 + 1) * 48 if isinstance(m, int) else (m - par) * 24 + 48))
                        pe.wait_ge(moe_out, m)
                        for k in range(2):
                            ins = nc.tensor.transpose(ps[:, 7, k * P:(k + 1) * P], XG[:, par, k * P:(k + 1) * P],
                                                      ident[:, :])
                        ins.then_inc(moe_T, 1)
                    Fg = it * 4 + s // GRP - 1
                    has_y = not (isinstance(Fg, int) and Fg < 0)
                    sp_ = (s - GRP) % SL
                    yb, f, hf = sp_ // PAIRS, (s % GRP) // 2, s % 2
                    if has_y and hf == 0:
                        if f == 0:
                            pe.wait_ge(scan_done, (Fg + 1) * GRP)
                        pe.wait_ge(y_evac, Fg * NFILL + f)
                    if has_y:
                        y_quarter((None, f), sp_, yb, 2 * hf, False)
                    if isM:
                        pe.wait_ge(moe_xT, m + 1)
                        for k in range(2):
                            ins = mm(ps[:, 7, 256:384], W1[:, par, k, :], XT[:, k, :], start=(k == 0), stop=(k == 1))
                        ins.then_inc(moe_L1, 1)
                    if has_y:
                        y_quarter((None, f), sp_, yb, 2 * hf + 1, hf == 1)
                    if isM:
                        pe.wait_ge(moe_sq, m + 1)
                        mm(ps[:, 7, 0:D], AS[:, :], W2[:, par, :], start=True, stop=True).then_inc(moe_L2, 1)

            body(0, False)
            with pe.Fori(1, BLK) as it:
                body(it, True)
            for f in range(NFILL):
                if f == 0:
                    pe.wait_ge(scan_done, BLK * SL)
                pe.wait_ge(y_evac, at_least_0((BLK * 4 - 1) * NFILL + f))
                for qq in range(4):
                    y_quarter((None, f), SL - GRP, 1, qq, qq == 3)

            pe.wait_ge(wend_in, 48)
            for q in range(4):
                for i4 in range(4):
                    n = 4 * q + i4
                    pe.wait_ge(up_relu, at_least_0(n - 1))
                    for k in range(2):
                        ins = mm(ps[:, n % 2, :], wup[:, k, i4 * P:(i4 + 1) * P], xnT[:, k, 512 * q:512 * q + 512],
                                 start=(k == 0), stop=(k == 1))
                    ins.then_inc(up_mm, 1)
                pe.wait_ge(up_sq, 4 * q + 4)
                pe.wait_ge(z2_ready, 4)
                for t in range(4 * q, 4 * q + 4):
                    pe.wait_ge(out_ready, at_least_0(t - 1))
                    b = t // 8
                    o = ps[:, 2 + t % 2, 0:D]
                    for i4 in range(4):
                        mm(o, H[:, i4 // 2, (i4 % 2) * 512 + (t % 4) * P:(i4 % 2) * 512 + (t % 4 + 1) * P], wdn[:, i4, :],
                           start=(i4 == 0), stop=False)
                    for h in range(2):
                        zv = H[:, 12 + 2 * h + b, (t % 8) * P:(t % 8 + 1) * P]
                        ins = mm(o, zv, wo[:, h, :], start=False, stop=(h == 1))
                    ins.then_inc(fin_mm, 1)


def kernel(**inputs):
    import concourse.bacc as _bacc
    from concourse.bass_utils import run_bass_kernel_spmd as _run

    a = {k.replace("L0_attn_", "").replace("L0_ffn_", ""): np.asarray(v) for k, v in inputs.items()}
    wp = a["x_proj_w"]
    wp = np.concatenate([wp[:RANK], wp[RANK:RANK + N], wp[RANK:RANK + N], wp[RANK + N:], wp[RANK + N:]])

    def rows(m):
        return m.reshape(2, P, -1).transpose(1, 0, 2)

    arrays = {
        "x_dram": a["x"].reshape(T, D),
        "xprojT_dram": rows(wp.T),
        "dtT_dram": a["dt_proj_w"].T,
        "vecs_dram": np.stack([a["norm_w"], a["norm_b"], a["dt_proj_b"], a["D_param"]]).reshape(4, 2, P).transpose(2, 1, 0),
        "A_l_dram": a["A_log"].reshape(P, 2, N).transpose(1, 2, 0).reshape(P, P),
        "outT_dram": rows(a["out_proj_w"].T),
        "gateT_dram": rows(a["gate_w"].T),
        "gbias_dram": a["gate_bias"],
        "w_up_dram": a["w_up_shared"],
        "w_down_dram": a["w_down_shared"],
        "w1_dram": a["w1_experts"],
        "w2_dram": a["w2_experts"],
    }
    arrays = {k: np.ascontiguousarray(v) for k, v in arrays.items()}
    nc = _bacc.Bacc("TRN2", target_bir_lowering=False, num_devices=1)
    args = [nc.dram_tensor(k, v.shape, mybir.dt.from_np(v.dtype), kind="ExternalInput").ap() for k, v in arrays.items()]
    args.append(nc.dram_tensor("out_dram", (T, D), mybir.dt.float32, kind="ExternalOutput").ap())
    state_space_and_experts(nc, *args)
    r = _run(nc, [arrays], core_ids=[0])
    return r.results[0]["out_dram"].reshape(a["x"].shape)
```

```python
import numpy as np
import concourse.bass as bass
from concourse import mybir
from contextlib import ExitStack

P = 128
T = 2048
NBATCH = 2
L = T // NBATCH
D = 256
N = 64
RANK = 128
PERIOD = 64
EXPERTS, TOPK, GROUPS, TOPG = 64, 6, 8, 4
INTER, SHARED = 128, 512
SCALE = 2.5
EPS = 1e-5
BIG = 1e30

TT = T // P
BLK = 8
CH = D // BLK
PAIRS = CH // 2
SL = NBATCH * PAIRS
GRP = 8
NFILL = 4
PRE = 1
NPRE = PRE * SL
MPI = 12
MBUF = 3
NPAIR = MPI * (BLK - PRE)
NMT = 2 * NPAIR
NXT = NMT + 4
DLEAD, GLEAD = 3, 3
assert NMT >= (T * TOPK + EXPERTS * (P - 1)) // P
PARTS = 3
PLOAD = 16 * (2 * PARTS + 1)
RING = 12


def state_space_and_experts(nc, x, xprojT, dtT, vecs, A_l, outT, gateT, gbias, w_up, w_down, w_exp, out):
    f32, bf16 = mybir.dt.float32, mybir.dt.bfloat16
    i32, u32 = mybir.dt.int32, mybir.dt.uint32
    ALU, ACT, AX = mybir.AluOpType, mybir.ActivationFunctionType, mybir.AxisListType

    ctx = ExitStack()
    with ctx:
        def sb(name, shape, dt=f32):
            return ctx.enter_context(nc.sbuf_tensor(name, shape, dt))

        def sem(name):
            return ctx.enter_context(nc.semaphore(name))

        parts_d = nc.dram_tensor("parts_d", (2, PARTS, D + CH, T), bf16, kind="Internal").ap()
        xg_d = nc.dram_tensor("xg_d", (NXT * P, D), f32, kind="Internal").ap()
        yg_d = nc.dram_tensor("yg_d", (NMT * P, D), f32, kind="Internal").ap()
        ys_d = nc.dram_tensor("ys_d", (D, NBATCH, L), f32, kind="Internal").ap()
        map_d = nc.dram_tensor("map_d", (2 * P, 1), u32, kind="Internal").ap()

        X = sb("X", [P, TT, D])
        AD = X[:, :, :].rearrange("p (a b) d -> p a (b d)", a=4)
        XN = sb("XN", [P, TT, D])
        xnT = sb("xnT", [P, 2, T])
        vec = sb("vec", [P, 2, 4])
        wn = sb("wn", [P, TT, TOPK])
        slot = sb("slot", [P, TOPK, TT], i32)
        emap = sb("emap", [1, 2 * P], u32)
        ident = sb("ident", [P, P])
        Aneg = sb("Aneg", [P, P + PAIRS])
        Acur = sb("Acur", [P, NBATCH, PAIRS])
        B2 = sb("B2", [P, T])
        CB = sb("CB", [P, NBATCH, PERIOD, 32])
        H = sb("H", [P, 2 * GRP, L])
        U = sb("U", [P, 4, L])
        GS = sb("GS", [P, 2, L])
        PD = sb("PD", [PARTS * CH, NBATCH, L], bf16)
        PG = sb("PG", [PARTS * CH, NBATCH, L], bf16)
        sel = sb("sel", [PARTS * CH, PAIRS, P], bf16)
        YS = sb("YS", [P, 2, 512])
        XG = sb("XG", [P, MBUF, 2, D])
        WE = sb("WE", [P, MBUF, 2, 2 * INTER + D])
        W1 = WE[:, :, :, 0:2 * INTER].rearrange("p a u (k i) -> p a u k i", k=2)
        W2 = WE[:, :, :, 2 * INTER:]
        XT = sb("XT", [P, 2, 2, P])
        RL = sb("RL", [P, 2, P])
        AS = sb("AS", [P, 2, P])
        YO = sb("YO", [P, 2, 2, D])
        ps = ctx.enter_context(nc.psum_tensor("ps", [P, 8, 512], f32))

        xn2T = H[:, 0:4, :].rearrange("p (h b) t -> p h (b t)", h=2)
        dpre = H[:, 4:6, :].rearrange("p b t -> p (b t)")
        Wproj = H[:, 6, 0:768].rearrange("p (k m) -> p k m", k=2)
        Wdt = H[:, 6, 768:1024]
        Wgate = U[:, 3, 0:128].rearrange("p (k m) -> p k m", k=2)
        z_t = H[:, 7, :]
        e_t = H[:, 8, :]
        l_t = H[:, 9, :]
        u_t = H[:, 10, :]
        dtg = H[:, 11:13, :]
        res = H[:, 13:15, :]
        prt = H[:, 15, :].bitcast(bf16).rearrange("p (a t) -> p a t", a=2)
        XN2 = H[:, 8:12, :].rearrange("p a (b c) -> p (a b) c", c=D)
        prt3 = GS[:, :, :].rearrange("p a t -> p (a t)").bitcast(bf16).rearrange("p (a t) -> p a t", a=4)
        wup = U[:, 2, :].rearrange("p (k m) -> p k m", k=2)
        wdn = U[:, 3, :].rearrange("p (k m) -> p k m", k=4)
        wo = GS[:, 0, 0:512].rearrange("p (k m) -> p k m", k=2)
        sc = H[:, 0, :]
        scb = H[:, 1, :]
        ra = H[:, 2, :]
        rb = H[:, 3, :]
        OH = H[:, 4:10, :]
        msel = H[:, 10, :]
        pos = H[:, 11, :]
        tot = H[:, 12, :]
        rc = H[:, 13, :]
        tri = H[:, 14, 0:64]
        iota_e = H[:, 14, 64:128]
        bias_b = H[:, 14, 128:192]
        small = H[:, 14, 192:1024]
        mbf = H[:, 15, 0:512].bitcast(bf16)
        ltri = H[:, 15, 512:576].bitcast(bf16)
        onesb = H[:, 15, 576:640].bitcast(bf16)

        st6 = sb("st6", [P, TT, 6])
        mv = sb("mv", [P, TT, 2])
        rstd = sb("rstd", [P, TT])
        rtmp = sb("rtmp", [P, 2, TT])

        x_in = sem("x_in")
        w_in = sem("w_in")
        w2_in = sem("w2_in")
        alog_in = sem("alog_in")
        wend_in = sem("wend_in")
        x_again = sem("x_again")
        zeros_stored = sem("zeros_stored")
        zero_set = sem("zero_set")
        consts = sem("consts")
        gate_exp = sem("gate_exp")
        stats_ready = sem("stats_ready")
        sqrt_ready = sem("sqrt_ready")
        xn_ready = sem("xn_ready")
        job_done = sem("job_done")
        xnT_evac = sem("xnT_evac")
        xn2T_evac = sem("xn2T_evac")
        logits_mm = sem("logits_mm")
        act_evac = sem("act_evac")
        dve_evac = sem("dve_evac")
        proj_mm = sem("proj_mm")
        a_exp = sem("a_exp")
        z_ready = sem("z_ready")
        e_ready = sem("e_ready")
        l_ready = sem("l_ready")
        dt_ready_p = sem("dt_ready_p")
        part1_ready = sem("part1_ready")
        part2_ready = sem("part2_ready")
        split_ready = sem("split_ready")
        parts_stored = sem("parts_stored")
        oh_ready = sem("oh_ready")
        prefix_mm = sem("prefix_mm")
        map_ready = sem("map_ready")
        map_stored = sem("map_stored")
        map_loaded = sem("map_loaded")
        slots_ready = sem("slots_ready")
        scattered = sem("scattered")
        chain = sem("chain")
        pchain = sem("pchain")
        aneg_ready = sem("aneg_ready")
        dt_bcast = sem("dt_bcast")
        g_bcast = sem("g_bcast")
        a_ready = sem("a_ready")
        g_dve = sem("g_dve")
        g_act = sem("g_act")
        gs_ready = sem("gs_ready")
        u_pool = sem("u_pool")
        scan_done = sem("scan_done")
        y_filled = sem("y_filled")
        y_evac = sem("y_evac")
        moe_T = sem("moe_T")
        moe_xT = sem("moe_xT")
        moe_L1 = sem("moe_L1")
        moe_relu = sem("moe_relu")
        moe_sq = sem("moe_sq")
        moe_L2 = sem("moe_L2")
        moe_out = sem("moe_out")
        gathered = sem("gathered")
        z2_ready = sem("z2_ready")
        up_mm = sem("up_mm")
        up_relu = sem("up_relu")
        up_sq = sem("up_sq")
        fin_mm = sem("fin_mm")
        fin_free = sem("fin_free")
        comb = sem("comb")
        out_ready = sem("out_ready")
        out_stored = sem("out_stored")
        s_parts = [sem(f"parts_loaded{b}") for b in range(2)]
        s_ys = [sem(f"y_stored{b}") for b in range(2)]
        s_mx = [sem(f"moe_loaded{b}") for b in range(MBUF)]
        s_mo = [sem(f"moe_stored{b}") for b in range(2)]
        s_yT = sem("yT_loaded")
        s_g = [sem(f"rows_gathered{b}") for b in range(RING)]
        s_os = [sem(f"out_stored{b}") for b in range(2)]

        def row(n):
            return H[:, 8 + (n % RING) // 4, (n % 4) * D:(n % 4 + 1) * D]

        def at_least_0(value):
            return max(value, 0) if isinstance(value, int) else value

        def early(it, c):
            return isinstance(it, int) and it * SL + c < NPRE

        def by_vector(it, c):
            return it * SL + c if early(it, c) else NPRE + (it - PRE) * (SL // 2) + c // 2

        def by_gpsimd(it, c):
            return 0 if early(it, c) else (it - PRE) * (SL // 2) + (c + 1) // 2

        def on_gpsimd(it, c):
            return not early(it, c) and c % 2 == 0

        block = ctx.enter_context(nc.Block())

        JOBS = ([("xnT", q, "act") for q in range(8)] + [("xn2T", q, "dve") for q in range(8)]
                + [("logit", q, "act") for q in range(2)] + [("B", q, "dve") for q in range(4)]
                + [("dpre", q, "act") for q in range(4)] + [("dt", q, "dve") for q in range(8)]
                + [("C", q, "dve") for q in range(2)]
                + [("prefix", q, "dve") for q in range(4)])
        JN = {(k, q): n for n, (k, q, _) in enumerate(JOBS)}

        STORED = [0, 6, 12, 24]

        def evac_no(n):
            return sum(1 for _, _, c in JOBS[:n + 1] if c == JOBS[n][2])

        @block.sync
        def _(sp):
            xv = x.rearrange("(k p) d -> p k d", p=P)
            for c in range(4):
                sp.dma_start(X[:, 4 * c:4 * c + 4, :], xv[:, 4 * c:4 * c + 4, :]).then_inc(x_in, 16)
            sp.dma_start(vec[:, :, :], vecs).then_inc(w_in, 16)
            sp.dma_start(Wgate, gateT).then_inc(w_in, 16)
            sp.dma_start(Wproj, xprojT).then_inc(w_in, 16)
            sp.dma_start(Wdt, dtT).then_inc(w_in, 16)
            sp.dma_start(Aneg[:, 0:P], A_l).then_inc(w_in, 16)
            sp.wait_ge(zero_set, 1)
            zr = xg_d.rearrange("(a p) d -> p a d", p=P)
            for c in range(0, NXT, 8):
                n = min(8, NXT - c)
                sp.dma_start(zr[:, c:c + n, :], CB[:, :, :, :].rearrange("p b r m -> p (b r m)")[:, 0:n * D].rearrange("p (a d) -> p a d", d=D))\
                    .then_inc(zeros_stored, 16)
            for q in range(4):
                h, b = q // 2, q % 2
                for kind in range(2):
                    sp.wait_ge(split_ready, 2 * q + kind + 1)
                    for a in range(PARTS):
                        src = (prt[:, kind, :] if a == 2 else prt3[:, 2 * kind + a, :])
                        sp.dma_start(parts_d[kind, a, h * P:(h + 1) * P, b * L:(b + 1) * L], src)\
                            .then_inc(parts_stored, 16)
                        if h == 1:
                            sp.dma_start(parts_d[kind, a, D:D + CH, b * L:(b + 1) * L], src[0:CH, :])\
                                .then_inc(parts_stored, 16)
            sp.wait_ge(parts_stored, 16 * (24 + 12))

            def load_parts(block_no, b):
                sp.dma_start(Acur[:, b, :], Aneg[:, bass.ds(block_no * PAIRS, PAIRS)]).then_inc(s_parts[b], 16)
                for kind, dst in ((0, PD), (1, PG)):
                    for a in range(PARTS):
                        sp.dma_start(dst[a * CH:(a + 1) * CH, b, :],
                                     parts_d[kind, a, bass.ds(block_no * CH, CH), b * L:(b + 1) * L])\
                            .then_inc(s_parts[b], 16)

            sp.wait_ge(aneg_ready, 2)
            load_parts(0, 0)
            sp.dma_start(bias_b, gbias.partition_broadcast(P)).then_inc(w2_in, 16)
            sp.wait_ge(map_ready, 1)
            for c in range(2):
                sp.dma_start(map_d[c * P:(c + 1) * P, :],
                             small[:, 820 + c:821 + c].bitcast(u32)).then_inc(map_stored, 16)
            sp.wait_ge(map_stored, 32)
            sp.dma_start(emap[:, :], map_d.rearrange("a b -> b a")).then_inc(map_loaded, 16)
            sp.wait_ge(map_loaded, 16)

            def load_expert(m, par):
                sp.dma_start(XG[:, par, :, :],
                             xg_d[bass.ds(m * 2 * P, 2 * P), :].rearrange("(u p) d -> p u d", p=P))\
                    .then_inc(s_mx[par], 16)
                for u in range(2):
                    e = sp.value_load(emap[0:1, bass.ds(m * 2 + u, 1)], min_val=0, max_val=EXPERTS - 1)
                    sp.dma_start(WE[:, par, u, :],
                                 w_exp[bass.ds(e, 1)].rearrange("e p n -> (e p) n")).then_inc(s_mx[par], 16)

            def store_fill(F, blk, s, f):
                G = F // NFILL if isinstance(F, int) else None
                par = f % 2
                sp.wait_ge(y_evac, F + 1)
                b, half = (s // PAIRS), (s // GRP) % 2
                for d2 in range(2):
                    dst = ys_d.rearrange("(k w g q) b (f j x) -> k w b f q j g x", k=BLK, w=2, q=2, f=NFILL, j=4)
                    dst = dst[bass.ds(blk, 1), half, b, f, d2].rearrange("k j g x -> (k j) g x")
                    src = YS[d2:96 + d2 + 1:32, par, :].rearrange("j (g x) -> j g x", g=GRP)
                    sp.dma_start(dst, src).then_inc(s_ys[par], 16)

            def body(it, moe):
                for s in range(SL):
                    if s % PAIRS == 0:
                        sp.wait_ge(scan_done, it * SL + s)
                        load_parts(it + s // PAIRS, 1 - s // PAIRS)
                    j = s // 2
                    if moe and s % 2 == 0 and j < MPI:
                        m = (it - PRE) * MPI + j
                        sp.wait_ge(moe_L2, m + 1)
                        load_expert(m + 2, (j + 2) % MBUF)
                    if s % 2 == 1:
                        f = (s % GRP) // 2
                        F = (it * 4 + s // GRP - 1) * NFILL + f
                        if not (isinstance(F, int) and F < 0):
                            ps_, pblk = ((s - GRP), it) if s >= GRP else (s - GRP + SL, it - 1)
                            store_fill(F, pblk, ps_, f)
                    if moe and s % 2 == 1 and 1 <= j <= MPI:
                        sp.wait_ge(moe_out, (it - PRE) * MPI + j + 1)
                        sp.dma_start(yg_d[bass.ds(((it - PRE) * MPI + j - 1) * 2 * P, 2 * P), :]
                                     .rearrange("(u p) d -> p u d", p=P),
                                     YO[:, (j - 1) % 2, :, :]).then_inc(s_mo[(j - 1) % 2], 16)

            for it in range(PRE):
                body(it, False)
            sp.wait_ge(scattered, 16 * TT * TOPK)
            for m in range(MBUF - 1):
                load_expert(m, m)
            with sp.Fori(PRE, BLK) as it:
                body(it, True)
            for f in range(NFILL):
                store_fill((BLK * 4 - 1) * NFILL + f, BLK - 1, SL - GRP, f)
            sp.wait_ge(scan_done, BLK * SL)
            sp.wait_ge(gs_ready, by_gpsimd(BLK, GLEAD))
            sp.wait_ge(u_pool, by_gpsimd(BLK, GLEAD - 1) + 2)
            sp.wait_ge(g_dve, by_vector(BLK, GLEAD))
            sp.dma_start(X[:, :, :], xv).then_inc(x_again, 16)
            sp.dma_start(wup, w_up.rearrange("(k p) m -> p k m", p=P)).then_inc(wend_in, 16)
            sp.dma_start(wdn, w_down.rearrange("(k p) m -> p k m", p=P)).then_inc(wend_in, 16)
            sp.dma_start(wo, outT).then_inc(wend_in, 16)
            for par in range(2):
                sp.wait_ge(s_ys[par], 2 * 16 * (BLK * 4 * NFILL // 2))
            for h in range(2):
                sp.dma_start(H[:, 4 + 2 * h:6 + 2 * h, :],
                             ys_d[h * P:(h + 1) * P, :, :]).then_inc(s_yT, 16)
            for k in range(TT):
                sp.wait_ge(out_ready, k + 1)
                sp.dma_start(out[k * P:(k + 1) * P, :], YO[:, k % 2, 0, :]).then_inc(s_os[k % 2], 16)
            for par in range(2):
                sp.wait_ge(s_os[par], 16 * TT // 2)
                sp.wait_ge(s_mo[par], 16 * (NPAIR // 2 + 1))
            for par in range(MBUF):
                sp.wait_ge(s_mx[par], 48 * len(range(par, NPAIR + MBUF - 1, MBUF)))
            sp.wait_ge(s_parts[0], PLOAD * (BLK + 1))

        @block.gpsimd
        def _(pool):
            nc.gpsimd.memset(CB[:, :, :, :], 0.0).then_inc(zero_set, 1)
            nc.gpsimd.memset(ident[:, :], 0.0).then_inc(pchain, 1)
            nc.gpsimd.memset(sel[:, :, :], 0.0).then_inc(pchain, 1)
            pool.wait_ge(pchain, 1)
            nc.gpsimd.affine_select(out=ident[:, :], in_=ident[:, :], compare_op=ALU.not_equal, fill=1.0,
                                    base=0, pattern=[[-1, P]], channel_multiplier=1).then_inc(consts, 1)
            pool.wait_ge(pchain, 2)
            for a in range(PARTS):
                pool.wait_ge(consts, a + 1)
                v = sel[a * CH:(a + 1) * CH, :, :].rearrange("p j (h n) -> p j h n", h=2)
                nc.gpsimd.affine_select(out=v, in_=v, compare_op=ALU.not_equal, fill=1.0, base=0,
                                        pattern=[[-2, PAIRS], [-1, 2], [0, N]], channel_multiplier=1)\
                    .then_inc(consts, 1)
            pool.wait_ge(consts, 4)
            pool.wait_ge(parts_stored, 16 * (24 + 12))
            pool.wait_ge(dt_ready_p, 8)
            nc.gpsimd.memset(tri, 1.0).then_inc(pchain, 1)
            nc.gpsimd.memset(ltri, 1.0).then_inc(pchain, 1)
            nc.gpsimd.memset(onesb, 1.0).then_inc(consts, 1)
            nc.gpsimd.memset(U[:, 0, 0:1], 0.0).then_inc(u_pool, 2)
            nc.gpsimd.memset(U[:, 0, 1:2], 0.0).then_inc(moe_L2, 1)
            nc.gpsimd.memset(U[:, 0, 2:3], 0.0).then_inc(moe_out, 1)
            nc.gpsimd.memset(U[:, 0, 3:4], 0.0).then_inc(s_mo[0], 16)
            nc.gpsimd.memset(U[:, 0, 4:5], 0.0).then_inc(s_mo[1], 16)
            nc.gpsimd.iota(iota_e, pattern=[[1, EXPERTS]], base=0, channel_multiplier=0,
                           allow_small_or_imprecise_dtypes=True).then_inc(consts, 1)
            nc.gpsimd.iota(small[:, 800:802], pattern=[[P, 2]], base=0, channel_multiplier=1,
                           allow_small_or_imprecise_dtypes=True).then_inc(consts, 1)
            pool.wait_ge(pchain, 4)
            tv = tri.rearrange("p (g h) -> p g h", g=GROUPS)
            nc.gpsimd.affine_select(out=tv, in_=tv, compare_op=ALU.is_gt, fill=0.0, base=0,
                                    pattern=[[1, GROUPS], [-1, GROUPS]], channel_multiplier=0)\
                .then_inc(consts, 1)
            nc.gpsimd.affine_select(out=ltri, in_=ltri, compare_op=ALU.is_gt, fill=0.0, base=0,
                                    pattern=[[1, P]], channel_multiplier=-1).then_inc(consts, 1)

            def scatter(k, t):
                pool.indirect_dma_start(xg_d, bass.IndirectOffsetOnAxis(ap=slot[:, k, t:t + 1].bitcast(u32), axis=0),
                                        XN[:, t, :], None).then_inc(scattered, 16)

            def body(it):
                for s in range(SL):
                    c = s + GLEAD - 1
                    if on_gpsimd(it, c):
                        pool.wait_ge(gs_ready, by_gpsimd(it, c) + 1)
                        pool.wait_ge(scan_done, it * SL + c - 3)
                        b = c // PAIRS % NBATCH
                        nc.gpsimd.tensor_tensor(U[:, c % 4, :], GS[:, c // 2 % 2, :], B2[:, b * L:(b + 1) * L],
                                                ALU.mult).then_inc(u_pool, 1)

            pool.wait_ge(slots_ready, 1)
            pool.wait_ge(zeros_stored, 16 * ((NXT + 7) // 8))
            for k in range(TOPK):
                for t in range(TT):
                    scatter(k, t)
            for it in range(PRE):
                body(it)
            with pool.Fori(PRE, BLK) as it:
                body(it)
            for par in range(2):
                pool.wait_ge(s_mo[par], 16 * (NPAIR // 2 + 1))
            pool.wait_ge(y_filled, BLK * 4 * NFILL)
            for t in range(TT):
                for k in range(TOPK):
                    n = t * TOPK + k
                    pool.wait_ge(comb, at_least_0(n - RING + 1))
                    pool.indirect_dma_start(row(n), None, yg_d,
                                            bass.IndirectOffsetOnAxis(ap=slot[:, k, t:t + 1].bitcast(u32), axis=0))\
                        .then_inc(s_g[n % RING], 16)

        @block.scalar
        def _(act):
            for ln in range(2):
                act.wait_ge(stats_ready, ln + 1)
                nc.scalar.activation(rstd[:, :], rtmp[:, 0, :], ACT.Sqrt).then_inc(sqrt_ready, 1)
            for q in range(8):
                act.wait_ge(job_done, JN["xnT", q] + 1)
                h, g4 = q % 2, q // 2
                nc.scalar.copy(xnT[:, h, 512 * g4:512 * g4 + 512], ps[:, JN["xnT", q] % 8, :])\
                    .then_inc(act_evac, 1)
            for q in range(2):
                n = JN["logit", q]
                act.wait_ge(job_done, n + 1)
                nc.scalar.activation(U[:, 2, q * 512:(q + 1) * 512], ps[:, n % 8, :], ACT.Exp, scale=-1.0)\
                    .then_inc(act_evac, 1)
            act.wait_ge(w_in, 80)
            nc.scalar.activation(Aneg[:, 0:P], Aneg[:, 0:P], ACT.Exp).then_inc(a_exp, 1)
            for q in range(4):
                n = JN["dpre", q]
                act.wait_ge(job_done, n + 1)
                nc.scalar.copy(dpre[:, 512 * q:512 * q + 512], ps[:, n % 8, :]).then_inc(act_evac, 1)
            for q in range(4):
                act.wait_ge(z_ready, q + 1)
                nc.scalar.activation(e_t, e_t, ACT.Exp).then_inc(e_ready, 1)
                act.wait_ge(e_ready, 2 * q + 1)
                nc.scalar.activation(l_t, e_t, ACT.Ln, bias=1.0).then_inc(e_ready, 1)
                for kind in range(2):
                    act.wait_ge(dt_ready_p, 2 * q + kind + 1)
                    act.wait_ge(parts_stored, 16 * STORED[q])
                    nc.scalar.copy(prt3[:, 2 * kind, :], dtg[:, kind, :]).then_inc(part1_ready, 1)
                for kind in range(2):
                    act.wait_ge(part2_ready, 2 * q + kind + 1)
                    nc.scalar.copy(prt3[:, 2 * kind + 1, :], res[:, kind, :]).then_inc(part1_ready, 1)

            act.wait_ge(parts_stored, 16 * (24 + 12))

            def decay(it, c):
                b, pair = c // PAIRS % NBATCH, c % PAIRS
                if pair == 0:
                    act.wait_ge(s_parts[b], (it + c // SL + 1) * PLOAD)
                act.wait_ge(scan_done, at_least_0(it * SL + c - 3))
                for k in range(2):
                    act.wait_ge(dt_bcast, 2 * (it * SL + c) + k + 1)
                    nc.scalar.activation(AD[:, c % 4, 512 * k:512 * k + 512], ps[:, k, :], ACT.Exp,
                                         scale=Acur[:, b, pair:pair + 1]).then_inc(a_ready, 1)

            def body(it, moe):
                for s in range(SL):
                    if moe and s % 2 == 0 and s // 2 < MPI:
                        act.wait_ge(moe_T, (it - PRE) * MPI + s // 2 + 1)
                        nc.scalar.copy(XT[:, :, :, :].rearrange("p u k t -> p (u k t)"), ps[:, 7, :]).then_inc(moe_xT, 1)
                    if moe and s % 2 == 1 and s // 2 < MPI:
                        act.wait_ge(moe_L1, (it - PRE) * MPI + s // 2 + 1)
                        nc.scalar.activation(RL[:, :, :], ps[:, 4, 0:2 * P].rearrange("p (u t) -> p u t", u=2), ACT.Relu)\
                            .then_inc(moe_relu, 1)
                    decay(it, s + DLEAD)
                    if s % 2 == 1:
                        f = (s % GRP) // 2
                        evac_fill((it * 4 + s // GRP - 1) * NFILL + f, f)
                    c = s + GLEAD
                    if on_gpsimd(it, c):
                        act.wait_ge(g_bcast, it * SL + c + 1)
                        act.wait_ge(u_pool, by_gpsimd(it, c) + 1)
                        nc.scalar.copy(GS[:, c // 2 % 2, :].rearrange("p (a c) -> p a c", a=2), ps[:, 2:4, :])\
                            .then_inc(gs_ready, 1)

            def evac_fill(F, f):
                if isinstance(F, int) and F < 0:
                    return
                act.wait_ge(y_filled, F + 1)
                act.wait_ge(s_ys[f % 2], at_least_0(32 * (F // 2) if isinstance(F, int) else (F - f % 2) * 16))
                nc.scalar.copy(YS[:, f % 2, :], ps[:, 6, :]).then_inc(y_evac, 1)

            for c in range(DLEAD):
                decay(0, c)
            for it in range(PRE):
                body(it, False)
            with act.Fori(PRE, BLK) as it:
                body(it, True)
            for f in range(NFILL):
                evac_fill((BLK * 4 - 1) * NFILL + f, f)
            act.wait_ge(u_pool, by_gpsimd(BLK, GLEAD - 1) + 2)
            act.wait_ge(g_dve, by_vector(BLK, GLEAD))
            for q in range(4):
                for it_ in range(4):
                    n = 4 * q + it_
                    act.wait_ge(up_mm, n + 1)
                    act.wait_ge(up_sq, at_least_0(n - 1))
                    nc.scalar.activation(U[:, n % 2, 0:512], ps[:, n % 2, :], ACT.Relu).then_inc(up_relu, 1)

        @block.vector
        def _(dve):
            count = [0]

            def link(ins):
                count[0] += 1
                ins.then_inc(chain, 1)
                dve.wait_ge(chain, count[0])

            V = nc.vector

            def layernorm(src, dst, ln):
                for k in range(TT):
                    if ln == 0 and k == 0:
                        dve.wait_ge(x_in, 64)
                    ins = V.bn_stats(st6[:, k, :], src[:, k, :])
                    if k == TT - 1:
                        link(ins)
                for k in range(TT):
                    ins = V.bn_aggr(mv[:, k, :], st6[:, k, :])
                link(ins)
                V.tensor_scalar(rtmp[:, 0, :], mv[:, :, 1], EPS, None, ALU.add).then_inc(stats_ready, 1)
                dve.wait_ge(sqrt_ready, ln + 1)
                link(V.reciprocal(rstd[:, :], rstd[:, :]))
                link(V.tensor_tensor(rtmp[:, 1, :], rstd[:, :], rstd[:, :], ALU.mult))
                link(V.tensor_tensor(rtmp[:, 1, :], rtmp[:, 1, :], rtmp[:, 0, :], ALU.mult))
                link(V.tensor_scalar(rtmp[:, 1, :], rtmp[:, 1, :], -0.5, 1.5, ALU.mult, ALU.add))
                link(V.tensor_tensor(rstd[:, :], rstd[:, :], rtmp[:, 1, :], ALU.mult))
                for k in range(TT):
                    ins = V.tensor_scalar(dst[:, k, :], src[:, k, :], mv[:, k, 0:1], rstd[:, k:k + 1],
                                          ALU.subtract, ALU.mult)
                ins.then_inc(xn_ready, 1)
                dve.wait_ge(xn_ready, ln + 1)

            layernorm(X, XN, 0)
            layernorm(XN, XN2, 1)
            dve.wait_ge(w_in, 80)
            for q in range(8):
                n = JN["xn2T", q]
                dve.wait_ge(job_done, n + 1)
                h, g4 = q % 2, q // 2
                V.tensor_scalar(xn2T[:, h, 512 * g4:512 * g4 + 512], ps[:, n % 8, :], vec[:, h, 0:1], vec[:, h, 1:2],
                                ALU.mult, ALU.add).then_inc(dve_evac, 1)
            for q in range(4):
                n = JN["B", q]
                dve.wait_ge(job_done, n + 1)
                V.tensor_copy(B2[:, 512 * q:512 * q + 512], ps[:, n % 8, :]).then_inc(dve_evac, 1)
            dve.wait_ge(a_exp, 1)
            V.tensor_scalar(Aneg[:, 0:P], Aneg[:, 0:P], -1.0, None, ALU.mult).then_inc(aneg_ready, 1)
            V.memset(Aneg[:, P:], 0.0).then_inc(aneg_ready, 1)

            for q in range(4):
                h, b = q // 2, q % 2
                for c in range(2):
                    n = JN["dt", 2 * q + c]
                    dve.wait_ge(job_done, n + 1)
                    ins = V.tensor_scalar(z_t[:, 512 * c:512 * c + 512], ps[:, n % 8, :], vec[:, h, 2:3], None, ALU.add)
                    ins.then_inc(dve_evac, 1)
                dve.wait_ge(dve_evac, evac_no(n))
                V.scalar_tensor_tensor(e_t, z_t, -1.0, z_t, ALU.mult, ALU.min).then_inc(z_ready, 1)
                dve.wait_ge(e_ready, 2 * q + 2)
                link(V.tensor_scalar(u_t, e_t, 1.0, None, ALU.add))
                link(V.scalar_tensor_tensor(u_t, u_t, -1.0, e_t, ALU.add, ALU.subtract))
                link(V.tensor_tensor(l_t, l_t, u_t, ALU.subtract))
                V.scalar_tensor_tensor(dtg[:, 0, :], z_t, 0.0, l_t, ALU.max, ALU.add).then_inc(dt_ready_p, 1)
                dve.wait_ge(dt_ready_p, 2 * q + 1)
                V.tensor_tensor(dtg[:, 1, :], dtg[:, 0, :], xn2T[:, h, b * L:(b + 1) * L], ALU.mult)\
                    .then_inc(dt_ready_p, 1)
                for kind in range(2):
                    dve.wait_ge(part1_ready, 4 * q + kind + 1)
                    dve.wait_ge(dt_ready_p, 2 * q + kind + 1)
                    V.tensor_tensor(res[:, kind, :], dtg[:, kind, :], prt3[:, 2 * kind, :], ALU.subtract)\
                        .then_inc(part2_ready, 1)
                for kind in range(2):
                    dve.wait_ge(part1_ready, 4 * q + 2 + kind + 1)
                    dve.wait_ge(parts_stored, 16 * STORED[q])
                    V.tensor_tensor(prt[:, kind, :], res[:, kind, :], prt3[:, 2 * kind + 1, :], ALU.subtract)\
                        .then_inc(split_ready, 1)

            dve.wait_ge(zeros_stored, 16 * ((NXT + 7) // 8))
            for b in range(2):
                n = JN["C", b]
                dve.wait_ge(job_done, n + 1)
                V.tensor_copy(CB[0:N, b, :, 0], ps[0:N, n % 8, 0:PERIOD])
                V.tensor_copy(CB[N:P, b, :, 1], ps[N:P, n % 8, 0:PERIOD]).then_inc(dve_evac, 1)

            dve.wait_ge(split_ready, 8)
            dve.wait_ge(act_evac, evac_no(JN["dpre", 3]))
            dve.wait_ge(w2_in, 16)
            dve.wait_ge(consts, 9)
            dve.wait_ge(parts_stored, 16 * 36)
            t8 = lambda a: a.rearrange("p (g e) -> p g e", e=8)
            t64 = lambda a: a.rearrange("p (t e) -> p t e", e=EXPERTS)
            g1, g2, g3, gs, pen = (small[:, 128 * n:128 * n + 128] for n in range(5))
            link(V.tensor_scalar(sc, U[:, 2, :], 1.0, None, ALU.add))
            link(V.reciprocal(sc, sc))
            link(V.tensor_tensor(t64(scb), t64(sc), bias_b.unsqueeze(1).broadcast_to((P, TT, EXPERTS)), ALU.add))
            bc8 = lambda a: a.unsqueeze(2).broadcast_to((P, P, 8))
            link(V.tensor_reduce(g1, t8(scb), AX.X, ALU.max))
            link(V.tensor_tensor(t8(ra), t8(scb), bc8(g1), ALU.is_equal))
            V.tensor_reduce(g2, t8(ra), AX.X, ALU.add)
            link(V.scalar_tensor_tensor(rb, ra, -BIG, scb, ALU.mult, ALU.add))
            V.tensor_reduce(g3, t8(rb), AX.X, ALU.max)
            link(V.tensor_scalar(g2, g2, 1.5, -BIG, ALU.is_lt, ALU.mult))
            link(V.tensor_tensor(g2, g2, g1, ALU.add))
            link(V.tensor_tensor(g3, g3, g2, ALU.max))
            link(V.tensor_tensor(gs, g1, g3, ALU.add))
            v3 = lambda a: a.rearrange("p (t g h) -> p t g h", g=GROUPS, h=GROUPS)
            gsv = gs.rearrange("p (t g) -> p t g", g=GROUPS)
            gh = gsv.unsqueeze(2).broadcast_to((P, TT, GROUPS, GROUPS))
            gg = gsv.unsqueeze(3).broadcast_to((P, TT, GROUPS, GROUPS))
            link(V.tensor_tensor(v3(rb), gh, gg, ALU.is_equal))
            link(V.tensor_tensor(t64(rb), t64(rb), tri.unsqueeze(1).broadcast_to((P, TT, 64)), ALU.mult))
            link(V.tensor_tensor(v3(ra), gh, gg, ALU.is_gt))
            link(V.tensor_tensor(ra, ra, rb, ALU.add))
            link(V.tensor_reduce(g2, t8(ra), AX.X, ALU.add))
            link(V.tensor_scalar(pen, g2, TOPG - 0.5, BIG, ALU.is_lt, ALU.mult))
            link(V.tensor_scalar(pen, pen, -BIG, None, ALU.add))
            link(V.tensor_tensor(t8(scb), t8(scb), bc8(pen), ALU.add))
            top = g1.rearrange("p (t e) -> p t e", e=8)
            idx = g2.bitcast(u32).rearrange("p (t e) -> p t e", e=8)
            idf = g3.rearrange("p (t e) -> p t e", e=8)
            for t in range(TT):
                ins = V.max(top[:, t, :], t64(scb)[:, t, :])
            link(ins)
            for t in range(TT):
                ins = V.max_index(idx[:, t, :], top[:, t, :], t64(scb)[:, t, :])
            link(ins)
            link(V.tensor_copy(idf, idx))
            iob = iota_e.unsqueeze(1).broadcast_to((P, TT, EXPERTS))
            for k in range(TOPK):
                link(V.tensor_tensor(t64(OH[:, k, :]), iob, idf[:, :, k:k + 1].broadcast_to((P, TT, EXPERTS)),
                                     ALU.is_equal))
                link(V.tensor_tensor(ra, OH[:, k, :], sc, ALU.mult))
                link(V.tensor_reduce(wn[:, :, k], t64(ra), AX.X, ALU.add))
                if k == 1:
                    link(V.tensor_tensor(msel, OH[:, 0, :], OH[:, 1, :], ALU.add))
                elif k > 1:
                    link(V.tensor_tensor(msel, msel, OH[:, k, :], ALU.add))
            V.tensor_copy(mbf, msel).then_inc(oh_ready, 1)
            wsum = small[:, 640:656]
            link(V.tensor_reduce(wsum, wn[:, :, :], AX.X, ALU.add))
            link(V.tensor_scalar(wsum, wsum, 1e-20, None, ALU.add))
            link(V.reciprocal(wsum, wsum))
            link(V.tensor_scalar(wsum, wsum, SCALE, None, ALU.mult))
            link(V.tensor_tensor(wn[:, :, :], wn[:, :, :], wsum.unsqueeze(2).broadcast_to((P, TT, TOPK)), ALU.mult))
            for q in range(4):
                n = JN["prefix", q]
                dve.wait_ge(job_done, n + 1)
                dst = pos if q < 2 else tot
                V.tensor_copy(dst[:, 512 * (q % 2):512 * (q % 2) + 512], ps[:, n % 8, :]).then_inc(dve_evac, 1)
            dve.wait_ge(dve_evac, evac_no(JN["prefix", 3]))
            run = t64(rb)
            link(V.tensor_copy(run[:, 0, :], t64(tot)[:, 0, :]))
            for t in range(1, TT):
                link(V.tensor_tensor(run[:, t, :], run[:, t - 1, :], t64(tot)[:, t, :], ALU.add))
            link(V.tensor_tensor(t64(pos)[:, 1:, :], t64(pos)[:, 1:, :], run[:, :TT - 1, :], ALU.add))
            nt = rc[:, 0:64]
            nti = rc[:, 64:128].bitcast(i32)
            incl = rc[:, 128:192]
            one = rc[:, 192:256]
            V.memset(one, 1.0)
            link(V.tensor_scalar(nt, run[:, TT - 1, :], float(P - 1), None, ALU.add))
            link(V.tensor_copy(nti, nt))
            link(V.tensor_scalar(nti, nti, 7, None, ALU.logical_shift_right))
            link(V.tensor_copy(nt, nti))
            link(V.tensor_tensor_scan(incl, one, nt, 0.0, ALU.mult, ALU.add))
            link(V.tensor_tensor(nt, incl, nt, ALU.subtract))
            link(V.tensor_scalar(nt, nt, float(P), None, ALU.mult))
            link(V.tensor_tensor(t64(pos), t64(pos), nt.unsqueeze(1).broadcast_to((P, TT, EXPERTS)), ALU.add))
            for c in range(2):
                link(V.tensor_scalar(one, incl, small[:, 800 + c:801 + c], None, ALU.is_le))
                link(V.tensor_reduce(small[:, 810 + c:811 + c], one, AX.X, ALU.add))
            link(V.tensor_scalar(small[:, 810:812], small[:, 810:812], float(EXPERTS - 1), None, ALU.min))
            V.tensor_copy(small[:, 820:822].bitcast(u32), small[:, 810:812]).then_inc(map_ready, 1)
            for k in range(TOPK):
                link(V.tensor_tensor(ra, OH[:, k, :], pos, ALU.mult))
                link(V.tensor_reduce(rc[:, 256 + 16 * k:272 + 16 * k], t64(ra), AX.X, ALU.add))
            V.tensor_copy(slot[:, :, :], rc[:, 256:256 + 96].rearrange("p (k t) -> p k t", k=TOPK))\
                .then_inc(slots_ready, 1)
            dve.wait_ge(map_stored, 32)
            dve.wait_ge(slots_ready, 1)

            def product(it, c):
                b = c // PAIRS % NBATCH
                dve.wait_ge(g_bcast, it * SL + c + 1)
                V.tensor_tensor(U[:, c % 4, :].rearrange("p (a c) -> p a c", a=2), ps[:, 2:4, :],
                                B2[:, b * L:(b + 1) * L].rearrange("p (a c) -> p a c", a=2), ALU.mult)\
                    .then_inc(g_dve, 1)

            def scan(it, s):
                if s % GRP == 0:
                    dve.wait_ge(y_filled, at_least_0((it * 4 + s // GRP - 1) * NFILL))
                if on_gpsimd(it, s):
                    dve.wait_ge(u_pool, by_gpsimd(it, s) + 3)
                else:
                    dve.wait_ge(g_dve, by_vector(it, s) + 1)
                dve.wait_ge(a_ready, 2 * (it * SL + s + 1))
                V.tensor_tensor_scan(H[:, (s // GRP % 2) * GRP + s % GRP, :],
                                     AD[:, s % 4, :], U[:, s % 4, :], 0.0, ALU.mult, ALU.add).then_inc(scan_done, 1)

            def body(it, moe):
                for s in range(SL):
                    if s % 2 == 0:
                        scan(it, s)
                        scan(it, s + 1)
                    j = s // 2
                    m = (it - PRE) * MPI + j
                    if not on_gpsimd(it, s + GLEAD):
                        product(it, s + GLEAD)
                    if moe and s % 2 == 1 and 1 <= j <= MPI:
                        dve.wait_ge(moe_L2, m + 1)
                        dve.wait_ge(s_mo[(j - 1) % 2], (m - 1 - (j - 1) % 2) * 8 + 16)
                        V.tensor_copy(YO[:, (j - 1) % 2, :, :].rearrange("p u d -> p (u d)"), ps[:, 5, :])\
                            .then_inc(moe_out, 1)
                    if moe and s % 2 == 1 and j < MPI:
                        dve.wait_ge(moe_relu, m + 1)
                        V.tensor_tensor(AS[:, :, :], RL[:, :, :], RL[:, :, :], ALU.mult).then_inc(moe_sq, 1)

            for c in range(GLEAD):
                product(0, c)
            for it in range(PRE):
                body(it, False)
            with dve.Fori(PRE, BLK) as it:
                body(it, True)

            dve.wait_ge(s_yT, 32)
            dve.wait_ge(x_again, 16)
            for h in range(2):
                for b in range(2):
                    yv = H[:, 4 + 2 * h + b, :].rearrange("p (r c) -> p r c", r=PERIOD)
                    xv = xnT[:, h, b * L:(b + 1) * L].rearrange("p (c r) -> p r c", r=PERIOD)
                    zv = H[:, 12 + 2 * h + b, :].rearrange("p (c r) -> p r c", r=PERIOD)
                    V.scalar_tensor_tensor(zv, xv, vec[:, h, 3:4], yv, ALU.mult, ALU.add).then_inc(z2_ready, 1)
            for q in range(4):
                for i4 in range(4):
                    n = 4 * q + i4
                    dve.wait_ge(up_relu, n + 1)
                    V.tensor_tensor(H[:, i4 // 2, (i4 % 2) * 512:(i4 % 2) * 512 + 512], U[:, n % 2, 0:512],
                                    U[:, n % 2, 0:512], ALU.mult).then_inc(up_sq, 1)
                for t in range(4 * q, 4 * q + 4):
                    for k in range(TOPK):
                        n = t * TOPK + k
                        dve.wait_ge(s_g[n % RING], 16 * (n // RING + 1))
                        if n:
                            dve.wait_ge(comb, n)
                        V.scalar_tensor_tensor(X[:, t, :], row(n), wn[:, t, k:k + 1], X[:, t, :], ALU.mult, ALU.add)\
                            .then_inc(comb, 1)
                    dve.wait_ge(comb, TOPK * (t + 1))
                    dve.wait_ge(fin_mm, t + 1)
                    if t < 2:
                        dve.wait_ge(s_mo[t % 2], 16 * (NPAIR // 2 + 1))
                    else:
                        dve.wait_ge(s_os[t % 2], 16 * (t // 2))
                    V.tensor_tensor(YO[:, t % 2, 0, :], ps[:, 2 + t % 2, 0:D], X[:, t, :], ALU.add)\
                        .then_inc(out_ready, 1)

        @block.tensor
        def _(pe):
            mm = nc.tensor.matmul
            for n, (kind, q, _) in enumerate(JOBS):
                bank = ps[:, n % 8, :]
                if n >= 8 and JOBS[n - 8][2] == "act":
                    pe.wait_ge(act_evac, evac_no(n - 8))
                elif n >= 8:
                    pe.wait_ge(dve_evac, evac_no(n - 8))
                if kind in ("xnT", "xn2T"):
                    if q == 0:
                        pe.wait_ge(consts, 1)
                        pe.wait_ge(xn_ready, 1 if kind == "xnT" else 2)
                    src = XN if kind == "xnT" else XN2
                    h, g4 = q % 2, q // 2
                    for j in range(4):
                        ins = nc.tensor.transpose(bank[:, j * P:(j + 1) * P], src[:, 4 * g4 + j, h * P:(h + 1) * P],
                                                  ident[:, :])
                elif kind == "logit":
                    if q == 0:
                        pe.wait_ge(w_in, 80)
                        pe.wait_ge(act_evac, 8)
                    for j in range(8):
                        t = 8 * q + j
                        for k in range(2):
                            ins = mm(bank[:, j * 64:(j + 1) * 64], xnT[:, k, t * P:(t + 1) * P], Wgate[:, k, :],
                                     start=(k == 0), stop=(k == 1))
                elif kind in ("B", "C", "dpre"):
                    if (kind, q) == ("B", 0):
                        pe.wait_ge(dve_evac, 8)
                    m0 = {"dpre": 0, "B": P, "C": 2 * P}[kind]
                    for k in range(2):
                        if kind == "C":
                            ins = mm(bank[:, 0:PERIOD], Wproj[:, k, m0:m0 + P], xn2T[:, k, q * L:q * L + PERIOD],
                                     start=(k == 0), stop=(k == 1))
                        else:
                            ins = mm(bank, Wproj[:, k, m0:m0 + P], xn2T[:, k, 512 * q:512 * q + 512],
                                     start=(k == 0), stop=(k == 1))
                elif kind == "dt":
                    if q == 0:
                        pe.wait_ge(act_evac, evac_no(JN["dpre", 3]))
                    h, tq = q // 4, q % 4
                    ins = mm(bank, Wdt[:, h * P:(h + 1) * P], dpre[:, 512 * tq:512 * tq + 512], start=True, stop=True)
                else:
                    if q == 0:
                        pe.wait_ge(oh_ready, 1)
                        pe.wait_ge(consts, 9)
                    ins = mm(bank, ltri if q < 2 else onesb, mbf[:, 512 * (q % 2):512 * (q % 2) + 512],
                             start=True, stop=True)
                ins.then_inc(job_done, 1)
            pe.wait_ge(dve_evac, evac_no(JN["prefix", 3]))
            pe.wait_ge(act_evac, evac_no(JN["dpre", 3]))

            def y_quarter(f, s, b, qq, last):
                hb = H[:, (s // GRP % 2) * GRP:(s // GRP % 2) * GRP + GRP, :]\
                    .rearrange("p g (c r) -> p g c r", r=PERIOD)
                for j in range(4):
                    r = f * 16 + j * 4 + qq
                    o = ps[32 * j:32 * j + 32, 6, :].rearrange("p (g a c) -> p g a c", g=GRP, a=4)[:, :, qq, :]
                    ins = mm(o, CB[:, b, r, :], hb[:, :, :, r], start=True, stop=True)
                if last:
                    ins.then_inc(y_filled, 1)

            def bcast_dt(it, c):
                b, pair = c // PAIRS % NBATCH, c % PAIRS
                if pair == 0:
                    pe.wait_ge(s_parts[b], (it + c // SL + 1) * PLOAD)
                for k in range(2):
                    pe.wait_ge(a_ready, at_least_0(2 * (it * SL + c - 1) + k + 1))
                    mm(ps[:, k, :], sel[:, pair, :], PD[:, b, 512 * k:512 * k + 512],
                       start=True, stop=True).then_inc(dt_bcast, 1)

            def bcast_g(it, c):
                b, pair = c // PAIRS % NBATCH, c % PAIRS
                if pair == 0:
                    pe.wait_ge(s_parts[b], (it + c // SL + 1) * PLOAD)
                if on_gpsimd(it, c - 1):
                    pe.wait_ge(gs_ready, by_gpsimd(it, c))
                else:
                    pe.wait_ge(g_dve, by_vector(it, c))
                for k in range(2):
                    ins = mm(ps[:, 2 + k, :], sel[:, pair, :], PG[:, b, 512 * k:512 * k + 512],
                             start=True, stop=True)
                ins.then_inc(g_bcast, 1)

            def body(it, moe):
                for s in range(SL):
                    j = s // 2
                    m = (it - PRE) * MPI + j
                    par = j % MBUF
                    if moe and s % 2 == 0 and j < MPI:
                        pe.wait_ge(s_mx[par], (m - par) * 16 + 48)
                        for n in range(4):
                            ins = nc.tensor.transpose(ps[:, 7, n * P:(n + 1) * P],
                                                      XG[:, par, n // 2, n % 2 * P:(n % 2 + 1) * P], ident[:, :])
                        ins.then_inc(moe_T, 1)
                    if moe and s % 2 == 1 and j < MPI:
                        pe.wait_ge(moe_xT, m + 1)
                        for u in range(2):
                            for k in range(2):
                                ins = mm(ps[:, 4, u * P:(u + 1) * P], W1[:, par, u, k, :], XT[:, u, k, :],
                                         start=(k == 0), stop=(k == 1))
                        ins.then_inc(moe_L1, 1)
                    bcast_dt(it, s + DLEAD)
                    Fg = it * 4 + s // GRP - 1
                    if not (isinstance(Fg, int) and Fg < 0):
                        yb, f, hf = (s - GRP) % SL // PAIRS, (s % GRP) // 2, s % 2
                        if (f, hf) == (0, 0):
                            pe.wait_ge(scan_done, (Fg + 1) * GRP)
                        if hf == 0:
                            pe.wait_ge(y_evac, Fg * NFILL + f)
                        y_quarter(f, (s - GRP) % SL, yb, 2 * hf, False)
                        y_quarter(f, (s - GRP) % SL, yb, 2 * hf + 1, hf == 1)
                    if moe and s % 2 == 0 and 1 <= j <= MPI:
                        pe.wait_ge(moe_sq, m)
                        pe.wait_ge(moe_out, m)
                        for u in range(2):
                            ins = mm(ps[:, 5, u * D:(u + 1) * D], AS[:, u, :], W2[:, (j - 1) % MBUF, u, :],
                                     start=True, stop=True)
                        ins.then_inc(moe_L2, 1)
                    bcast_g(it, s + GLEAD)

            for c in range(GLEAD):
                bcast_g(0, c)
            for c in range(DLEAD):
                bcast_dt(0, c)
            for it in range(PRE):
                body(it, False)
            with pe.Fori(PRE, BLK) as it:
                body(it, True)
            for f in range(NFILL):
                if f == 0:
                    pe.wait_ge(scan_done, BLK * SL)
                pe.wait_ge(y_evac, at_least_0((BLK * 4 - 1) * NFILL + f))
                for qq in range(4):
                    y_quarter(f, SL - GRP, 1, qq, qq == 3)

            pe.wait_ge(a_ready, 2 * (BLK * SL + DLEAD))
            pe.wait_ge(g_dve, by_vector(BLK, GLEAD))
            pe.wait_ge(gs_ready, by_gpsimd(BLK, GLEAD))
            pe.wait_ge(wend_in, 48)
            for q in range(4):
                for i4 in range(4):
                    n = 4 * q + i4
                    pe.wait_ge(up_relu, at_least_0(n - 1))
                    for k in range(2):
                        ins = mm(ps[:, n % 2, :], wup[:, k, i4 * P:(i4 + 1) * P], xnT[:, k, 512 * q:512 * q + 512],
                                 start=(k == 0), stop=(k == 1))
                    ins.then_inc(up_mm, 1)
                pe.wait_ge(up_sq, 4 * q + 4)
                pe.wait_ge(z2_ready, 4)
                for t in range(4 * q, 4 * q + 4):
                    pe.wait_ge(out_ready, at_least_0(t - 1))
                    b = t // 8
                    o = ps[:, 2 + t % 2, 0:D]
                    for i4 in range(4):
                        mm(o, H[:, i4 // 2, (i4 % 2) * 512 + (t % 4) * P:(i4 % 2) * 512 + (t % 4 + 1) * P], wdn[:, i4, :],
                           start=(i4 == 0), stop=False)
                    for h in range(2):
                        zv = H[:, 12 + 2 * h + b, (t % 8) * P:(t % 8 + 1) * P]
                        ins = mm(o, zv, wo[:, h, :], start=False, stop=(h == 1))
                    ins.then_inc(fin_mm, 1)


def kernel(**inputs):
    import concourse.bacc as _bacc
    from concourse.bass_utils import run_bass_kernel_spmd as _run

    a = {k.replace("L0_attn_", "").replace("L0_ffn_", ""): np.asarray(v) for k, v in inputs.items()}
    wp = a["x_proj_w"]
    wp = np.concatenate([wp[:RANK], wp[RANK:RANK + N], wp[RANK:RANK + N], wp[RANK + N:], wp[RANK + N:]])

    def rows(m):
        return m.reshape(2, P, -1).transpose(1, 0, 2)

    arrays = {
        "x_dram": a["x"].reshape(T, D),
        "xprojT_dram": rows(wp.T),
        "dtT_dram": a["dt_proj_w"].T,
        "vecs_dram": np.stack([a["norm_w"], a["norm_b"], a["dt_proj_b"], a["D_param"]]).reshape(4, 2, P).transpose(2, 1, 0),
        "A_l_dram": a["A_log"].reshape(P, 2, N).transpose(1, 2, 0).reshape(P, P),
        "outT_dram": rows(a["out_proj_w"].T),
        "gateT_dram": rows(a["gate_w"].T),
        "gbias_dram": a["gate_bias"],
        "w_up_dram": a["w_up_shared"],
        "w_down_dram": a["w_down_shared"],
        "w_exp_dram": np.concatenate([a["w1_experts"].reshape(EXPERTS, 2, P, INTER).transpose(0, 2, 1, 3)
                                      .reshape(EXPERTS, P, 2 * INTER), a["w2_experts"]], axis=2),
    }
    arrays = {k: np.ascontiguousarray(v) for k, v in arrays.items()}
    nc = _bacc.Bacc("TRN2", target_bir_lowering=False, num_devices=1)
    args = [nc.dram_tensor(k, v.shape, mybir.dt.from_np(v.dtype), kind="ExternalInput").ap() for k, v in arrays.items()]
    args.append(nc.dram_tensor("out_dram", (T, D), mybir.dt.float32, kind="ExternalOutput").ap())
    state_space_and_experts(nc, *args)
    r = _run(nc, [arrays], core_ids=[0])
    return r.results[0]["out_dram"].reshape(a["x"].shape)
```

```python
import numpy as np
import concourse.bass as bass
from concourse import mybir
from contextlib import ExitStack

P = 128
T = 2048
NBATCH = 2
L = T // NBATCH
D = 256
N = 64
RANK = 128
PERIOD = 64
EXPERTS, TOPK, GROUPS, TOPG = 64, 6, 8, 4
INTER, SHARED = 128, 512
SCALE = 2.5
EPS = 1e-5
BIG = 1e30

TT = T // P
BLK = 8
CH = D // BLK
PAIRS = CH // 2
SL = NBATCH * PAIRS
GRP = 8
NFILL = 4
PRE = 1
NPRE = PRE * SL
LATE = (BLK - 1) * SL + 3
MPI = 15
MBUF = 3
NPAIR = MPI * (BLK - 1 - PRE)
NMT = 2 * NPAIR
NXT = NMT + 4
DLEAD, GLEAD = 3, 3
assert LATE == (BLK - 1) * SL + GLEAD and NMT >= (T * TOPK + EXPERTS * (P - 1)) // P
PARTS = 3
PLOAD = 16 * (2 * PARTS + 1)
RING = 12


def state_space_and_experts(nc, x, xprojT, dtT, vecs, A_l, outT, gateT, gbias, w_up, w_down, w_exp, out):
    f32, bf16 = mybir.dt.float32, mybir.dt.bfloat16
    i32, u32 = mybir.dt.int32, mybir.dt.uint32
    ALU, ACT, AX = mybir.AluOpType, mybir.ActivationFunctionType, mybir.AxisListType

    ctx = ExitStack()
    with ctx:
        def sb(name, shape, dt=f32):
            return ctx.enter_context(nc.sbuf_tensor(name, shape, dt))

        def sem(name):
            return ctx.enter_context(nc.semaphore(name))

        parts_d = nc.dram_tensor("parts_d", (2, PARTS, D + CH, T), bf16, kind="Internal").ap()
        xg_d = nc.dram_tensor("xg_d", (NXT * P, D), f32, kind="Internal").ap()
        xs_d = nc.dram_tensor("xs_d", (T, D), f32, kind="Internal").ap()
        yg_d = nc.dram_tensor("yg_d", (NMT * P, D), f32, kind="Internal").ap()
        ys_d = nc.dram_tensor("ys_d", (D, NBATCH, L), f32, kind="Internal").ap()
        map_d = nc.dram_tensor("map_d", (2 * P, 1), u32, kind="Internal").ap()

        X = sb("X", [P, TT, D])
        AD = X[:, :, :].rearrange("p (a b) d -> p a (b d)", a=4)
        XN = sb("XN", [P, TT, D])
        xnT = sb("xnT", [P, 2, T])
        vec = sb("vec", [P, 2, 4])
        wn = sb("wn", [P, TT, TOPK])
        slot = sb("slot", [P, TOPK, TT], i32)
        emap = sb("emap", [1, 2 * P], u32)
        ident = sb("ident", [P, P])
        Aneg = sb("Aneg", [P, P + PAIRS])
        Acur = sb("Acur", [P, NBATCH, PAIRS])
        B2 = sb("B2", [P, T])
        CB = sb("CB", [P, NBATCH, PERIOD, 32])
        H = sb("H", [P, 2 * GRP, L])
        U = sb("U", [P, 4, L])
        GS = sb("GS", [P, 2, L])
        PD = sb("PD", [PARTS * CH, NBATCH, L], bf16)
        PG = sb("PG", [PARTS * CH, NBATCH, L], bf16)
        sel = sb("sel", [PARTS * CH, PAIRS, P], bf16)
        YS = sb("YS", [P, 2, 512])
        XG = sb("XG", [P, MBUF, 2, D])
        WE = sb("WE", [P, MBUF, 2, 2 * INTER + D])
        W1 = WE[:, :, :, 0:2 * INTER].rearrange("p a u (k i) -> p a u k i", k=2)
        W2 = WE[:, :, :, 2 * INTER:]
        XT = sb("XT", [P, 2, 2, P])
        RL = sb("RL", [P, 2, P])
        AS = sb("AS", [P, 2, P])
        YO = sb("YO", [P, MBUF, 2, D])
        ps = ctx.enter_context(nc.psum_tensor("ps", [P, 8, 512], f32))

        xn2T = H[:, 0:4, :].rearrange("p (h b) t -> p h (b t)", h=2)
        dpre = H[:, 4:6, :].rearrange("p b t -> p (b t)")
        Wproj = H[:, 6, 0:768].rearrange("p (k m) -> p k m", k=2)
        Wdt = H[:, 6, 768:1024]
        Wgate = U[:, 3, 0:128].rearrange("p (k m) -> p k m", k=2)
        z_t = H[:, 7, :]
        e_t = H[:, 8, :]
        l_t = H[:, 9, :]
        u_t = H[:, 10, :]
        dtg = H[:, 11:13, :]
        res = H[:, 13:15, :]
        prt = H[:, 15, :].bitcast(bf16).rearrange("p (a t) -> p a t", a=2)
        XN2 = H[:, 8:12, :].rearrange("p a (b c) -> p (a b) c", c=D)
        prt3 = GS[:, :, :].rearrange("p a t -> p (a t)").bitcast(bf16).rearrange("p (a t) -> p a t", a=4)
        wup = WE[:, 0, :, :]
        wdn = WE[:, 1, :, :].rearrange("p u (k m) -> p (u k) m", k=2)
        hid = [WE[:, 2, 0, :], WE[:, 2, 1, :], XG[:, 0, :, :].rearrange("p u d -> p (u d)"),
               XG[:, 1, :, :].rearrange("p u d -> p (u d)")]
        shared_out = [RL[:, :, :].rearrange("p u t -> p (u t)"), AS[:, :, :].rearrange("p u t -> p (u t)")]
        wo = GS[:, 0, 0:512].rearrange("p (k m) -> p k m", k=2)
        sc = U[:, 2, :]
        scb = U[:, 0, :]
        ra = U[:, 1, :]
        rb = H[:, 7, :]
        OH = [H[:, 8 + k // 2, k % 2 * 512:(k % 2 + 1) * 512].bitcast(bf16) for k in range(TOPK)]
        pos = H[:, 11, :]
        tot = H[:, 12, :]
        rc = H[:, 13, :]
        tri = H[:, 14, 0:64]
        iota_e = H[:, 14, 64:128]
        bias_b = H[:, 14, 128:192]
        small = H[:, 14, 192:1024]
        ltri = H[:, 15, 512:576].bitcast(bf16)
        onesb = H[:, 15, 576:640].bitcast(bf16)

        st6 = sb("st6", [P, TT, 6])
        mapv = sb("mapv", [P, 2], u32)
        mv = sb("mv", [P, TT, 2])
        rstd = sb("rstd", [P, TT])
        rtmp = sb("rtmp", [P, 2, TT])

        x_in = sem("x_in")
        w_in = sem("w_in")
        bias_in = sem("bias_in")
        alog_in = sem("alog_in")
        wend_in = sem("wend_in")
        wsh_in = sem("wsh_in")
        x_again = sem("x_again")
        sh_mm = sem("sh_mm")
        sh_copied = sem("sh_copied")
        sh_ready = sem("sh_ready")
        xs_stored = sem("xs_stored")
        zeros_stored = sem("zeros_stored")
        zero_set = sem("zero_set")
        consts = sem("consts")
        gate_exp = sem("gate_exp")
        stats_ready = sem("stats_ready")
        sqrt_ready = sem("sqrt_ready")
        xn_ready = sem("xn_ready")
        job_done = sem("job_done")
        xnT_evac = sem("xnT_evac")
        xn2T_evac = sem("xn2T_evac")
        logits_mm = sem("logits_mm")
        act_evac = sem("act_evac")
        dve_evac = sem("dve_evac")
        proj_mm = sem("proj_mm")
        a_exp = sem("a_exp")
        z_ready = sem("z_ready")
        e_ready = sem("e_ready")
        l_ready = sem("l_ready")
        dt_ready_p = sem("dt_ready_p")
        part1_ready = sem("part1_ready")
        part2_ready = sem("part2_ready")
        split_ready = sem("split_ready")
        parts_stored = sem("parts_stored")
        oh_ready = sem("oh_ready")
        prefix_mm = sem("prefix_mm")
        map_ready = sem("map_ready")
        map_stored = sem("map_stored")
        map_loaded = sem("map_loaded")
        slots_ready = sem("slots_ready")
        scattered = sem("scattered")
        chain = sem("chain")
        pchain = sem("pchain")
        aneg_ready = sem("aneg_ready")
        dt_bcast = sem("dt_bcast")
        g_bcast = sem("g_bcast")
        a_ready = sem("a_ready")
        g_dve = sem("g_dve")
        g_act = sem("g_act")
        gs_ready = sem("gs_ready")
        u_pool = sem("u_pool")
        scan_done = sem("scan_done")
        y_filled = sem("y_filled")
        y_evac = sem("y_evac")
        moe_T = sem("moe_T")
        moe_xT = sem("moe_xT")
        moe_L1 = sem("moe_L1")
        moe_relu = sem("moe_relu")
        moe_sq = sem("moe_sq")
        moe_L2 = sem("moe_L2")
        moe_out = sem("moe_out")
        z2_ready = sem("z2_ready")
        up_mm = sem("up_mm")
        up_relu = sem("up_relu")
        up_sq = sem("up_sq")
        fin_mm = sem("fin_mm")
        fin_free = sem("fin_free")
        comb = sem("comb")
        out_ready = sem("out_ready")
        s_parts = [sem(f"parts_loaded{b}") for b in range(2)]
        s_ys = [sem(f"y_stored{b}") for b in range(2)]
        s_mx = [sem(f"moe_loaded{b}") for b in range(MBUF)]
        s_mo = [sem(f"moe_stored{b}") for b in range(MBUF)]
        s_yT = sem("yT_loaded")
        s_g = [sem(f"rows_gathered{b}") for b in range(RING)]
        s_os = [sem(f"out_stored{b}") for b in range(2)]

        def row(n):
            return WE[:, n % RING // 4, n % 4 // 2, n % 2 * D:(n % 2 + 1) * D]

        def at_least_0(value):
            return max(value, 0) if isinstance(value, int) else value

        def vector_tile(i):
            return i < NPRE or i >= LATE or i % 2 == 1

        def by_vector(it, c):
            if isinstance(it, int):
                return sum(vector_tile(i) for i in range(it * SL + c))
            return NPRE + (it - PRE) * (SL // 2) + c // 2

        def by_gpsimd(it, c):
            if isinstance(it, int):
                return it * SL + c - by_vector(it, c)
            return (it - PRE) * (SL // 2) + (c + 1) // 2

        def on_gpsimd(it, c):
            return not vector_tile(it * SL + c) if isinstance(it, int) else c % 2 == 0

        def two_g(it, c):
            return isinstance(it, int) and (it * SL + c < NPRE or it * SL + c >= LATE)

        def g_bank(it, c):
            return 2 + 2 * (it * SL + c) % 4 if two_g(it, c) else 2

        block = ctx.enter_context(nc.Block())

        JOBS = ([("xnT", q, "act") for q in range(8)] + [("logit", q, "act") for q in range(2)]
                + [("xn2T", q, "dve") for q in range(8)] + [("B", q, "dve") for q in range(4)]
                + [("dpre", q, "act") for q in range(4)] + [("C", q, "dve") for q in range(2)]
                + [("prefix", q, "dve") for q in range(4)] + [("dt", q, "dve") for q in range(8)])
        JN = {(k, q): n for n, (k, q, _) in enumerate(JOBS)}

        def job_bank(n):
            return n % 8 if n < 32 else 2 + (n - 32) % 6

        assert JN["dpre", 3] == 25 and JN["dt", 0] == 32
        SH_CUT = (14, 28, 2 * TT)

        STORED = [0, 6, 12, 24]

        def evac_no(n):
            return sum(1 for _, _, c in JOBS[:n + 1] if c == JOBS[n][2])

        @block.sync
        def _(sp):
            xv = x.rearrange("(k p) d -> p k d", p=P)
            for c in range(4):
                sp.dma_start(X[:, 4 * c:4 * c + 4, :], xv[:, 4 * c:4 * c + 4, :]).then_inc(x_in, 16)
            sp.dma_start(vec[:, :, :], vecs).then_inc(w_in, 16)
            sp.dma_start(Wgate, gateT).then_inc(w_in, 16)
            sp.dma_start(Wproj, xprojT).then_inc(w_in, 16)
            sp.dma_start(Wdt, dtT).then_inc(w_in, 16)
            sp.dma_start(Aneg[:, 0:P], A_l).then_inc(w_in, 16)
            sp.dma_start(wup, w_up.rearrange("(k p) m -> p k m", p=P)).then_inc(wsh_in, 16)
            sp.dma_start(wdn, w_down.rearrange("(k p) m -> p k m", p=P)).then_inc(wsh_in, 16)
            sp.dma_start(bias_b, gbias.partition_broadcast(P)).then_inc(bias_in, 16)
            sp.wait_ge(zero_set, 1)
            zr = xg_d.rearrange("(a p) d -> p a d", p=P)
            for c in range(0, NXT, 8):
                n = min(8, NXT - c)
                sp.dma_start(zr[:, c:c + n, :], CB[:, :, :, :].rearrange("p b r m -> p (b r m)")[:, 0:n * D].rearrange("p (a d) -> p a d", d=D))\
                    .then_inc(zeros_stored, 16)
            sp.wait_ge(map_ready, 1)
            for c in range(2):
                sp.dma_start(map_d[c * P:(c + 1) * P, :],
                             mapv[:, c:c + 1]).then_inc(map_stored, 16)
            sp.wait_ge(map_stored, 32)
            sp.dma_start(emap[:, :], map_d.rearrange("a b -> b a")).then_inc(map_loaded, 16)
            sp.wait_ge(map_loaded, 16)
            def load_parts(block_no, b):
                sp.dma_start(Acur[:, b, :], Aneg[:, bass.ds(block_no * PAIRS, PAIRS)]).then_inc(s_parts[b], 16)
                for kind, dst in ((0, PD), (1, PG)):
                    for a in range(PARTS):
                        sp.dma_start(dst[a * CH:(a + 1) * CH, b, :],
                                     parts_d[kind, a, bass.ds(block_no * CH, CH), b * L:(b + 1) * L])\
                            .then_inc(s_parts[b], 16)

            for q in range(4):
                h, b = q // 2, q % 2
                if q == 3:
                    sp.wait_ge(sh_ready, TT)
                    sp.dma_start(xs_d.rearrange("(k p) d -> p k d", p=P), X[:, :, :]).then_inc(xs_stored, 16)
                if q == 2:
                    sp.wait_ge(parts_stored, 16 * STORED[2])
                    sp.wait_ge(aneg_ready, 2)
                    load_parts(0, 0)
                for kind in range(2):
                    sp.wait_ge(split_ready, 2 * q + kind + 1)
                    for a in range(PARTS):
                        src = (prt[:, kind, :] if a == 2 else prt3[:, 2 * kind + a, :])
                        sp.dma_start(parts_d[kind, a, h * P:(h + 1) * P, b * L:(b + 1) * L], src)\
                            .then_inc(parts_stored, 16)
                        if h == 1:
                            sp.dma_start(parts_d[kind, a, D:D + CH, b * L:(b + 1) * L], src[0:CH, :])\
                                .then_inc(parts_stored, 16)
            sp.wait_ge(parts_stored, 16 * (24 + 12))

            def load_expert(m, par):
                sp.dma_start(XG[:, par, :, :],
                             xg_d[bass.ds(m * 2 * P, 2 * P), :].rearrange("(u p) d -> p u d", p=P))\
                    .then_inc(s_mx[par], 16)
                for u in range(2):
                    e = sp.value_load(emap[0:1, bass.ds(m * 2 + u, 1)], min_val=0, max_val=EXPERTS - 1)
                    sp.dma_start(WE[:, par, u, :],
                                 w_exp[bass.ds(e, 1)].rearrange("e p n -> (e p) n")).then_inc(s_mx[par], 16)

            def store_fill(F, blk, s, f):
                par = f % 2
                sp.wait_ge(y_evac, F + 1)
                b, half = (s // PAIRS), (s // GRP) % 2
                for d2 in range(2):
                    dst = ys_d.rearrange("(k w g q) b (f j x) -> k w b f q j g x", k=BLK, w=2, q=2, f=NFILL, j=4)
                    dst = dst[bass.ds(blk, 1), half, b, f, d2].rearrange("k j g x -> (k j) g x")
                    src = YS[d2:96 + d2 + 1:32, par, :].rearrange("j (g x) -> j g x", g=GRP)
                    sp.dma_start(dst, src).then_inc(s_ys[par], 16)

            def body(it, moe):
                for s in range(SL):
                    if s % PAIRS == 0:
                        sp.wait_ge(scan_done, it * SL + s)
                        load_parts(it + s // PAIRS, 1 - s // PAIRS)
                    j = s // 2
                    if moe and s % 2 == 0 and j < MPI:
                        m = (it - PRE) * MPI + j
                        sp.wait_ge(moe_L2, m + 1)
                        load_expert(m + 2, (j + 2) % MBUF)
                    if s % 2 == 1:
                        f = (s % GRP) // 2
                        F = (it * 4 + s // GRP - 1) * NFILL + f
                        if not (isinstance(F, int) and F < 0):
                            ps_, pblk = ((s - GRP), it) if s >= GRP else (s - GRP + SL, it - 1)
                            store_fill(F, pblk, ps_, f)
                    if moe and s % 2 == 1 and 1 <= j <= MPI:
                        sp.wait_ge(moe_out, (it - PRE) * MPI + j + 1)
                        sp.dma_start(yg_d[bass.ds(((it - PRE) * MPI + j - 1) * 2 * P, 2 * P), :]
                                     .rearrange("(u p) d -> p u d", p=P),
                                     YO[:, (j - 1) % MBUF, :, :]).then_inc(s_mo[(j - 1) % MBUF], 16)

            for it in range(PRE):
                body(it, False)
            sp.wait_ge(scattered, 16 * TT * TOPK)
            for m in range(MBUF - 1):
                load_expert(m, m)
            with sp.Fori(PRE, BLK - 1) as it:
                body(it, True)
            sp.dma_start(XN[:, :, :], xs_d.rearrange("(k p) d -> p k d", p=P)).then_inc(x_again, 16)
            sp.wait_ge(gs_ready, by_gpsimd(BLK, 0))
            sp.wait_ge(u_pool, by_gpsimd(BLK, 0) + 2)
            sp.dma_start(wo, outT).then_inc(wend_in, 16)
            body(BLK - 1, False)
            sp.wait_ge(y_filled, (BLK * 4 - 1) * NFILL)
            for par in range(2):
                sp.wait_ge(s_ys[par], 32 * (BLK * 4 - 1) * NFILL // 2)
            sp.dma_start(H[:, 4:6, :], ys_d[0:P, :, :]).then_inc(s_yT, 16)
            for f in range(NFILL):
                store_fill((BLK * 4 - 1) * NFILL + f, BLK - 1, SL - GRP, f)
            for par in range(2):
                sp.wait_ge(s_ys[par], 2 * 16 * (BLK * 4 * NFILL // 2))
            sp.wait_ge(s_yT, 16)
            sp.dma_start(H[:, 6:8, :], ys_d[P:2 * P, :, :]).then_inc(s_yT, 16)
            for k in range(TT):
                sp.wait_ge(out_ready, k + 1)
                sp.dma_start(out[k * P:(k + 1) * P, :], YO[:, k % 2, 0, :]).then_inc(s_os[k % 2], 16)
            for par in range(2):
                sp.wait_ge(s_os[par], 16 * TT // 2)
            for par in range(MBUF):
                sp.wait_ge(s_mo[par], 16 * (NPAIR // MBUF + 1))
                sp.wait_ge(s_mx[par], 48 * len(range(par, NPAIR + MBUF - 1, MBUF)))
            sp.wait_ge(s_parts[0], PLOAD * (BLK + 1))

        @block.gpsimd
        def _(pool):
            nc.gpsimd.memset(CB[:, :, :, :], 0.0).then_inc(zero_set, 1)
            nc.gpsimd.memset(ident[:, :], 0.0).then_inc(pchain, 1)
            nc.gpsimd.memset(sel[:, :, :], 0.0).then_inc(pchain, 1)
            pool.wait_ge(pchain, 1)
            nc.gpsimd.affine_select(out=ident[:, :], in_=ident[:, :], compare_op=ALU.not_equal, fill=1.0,
                                    base=0, pattern=[[-1, P]], channel_multiplier=1).then_inc(consts, 1)
            pool.wait_ge(pchain, 2)
            for a in range(PARTS):
                pool.wait_ge(consts, a + 1)
                v = sel[a * CH:(a + 1) * CH, :, :].rearrange("p j (h n) -> p j h n", h=2)
                nc.gpsimd.affine_select(out=v, in_=v, compare_op=ALU.not_equal, fill=1.0, base=0,
                                        pattern=[[-2, PAIRS], [-1, 2], [0, N]], channel_multiplier=1)\
                    .then_inc(consts, 1)
            pool.wait_ge(consts, 4)
            nc.gpsimd.memset(tri, 1.0).then_inc(pchain, 1)
            nc.gpsimd.memset(ltri, 1.0).then_inc(pchain, 1)
            nc.gpsimd.memset(onesb, 1.0).then_inc(consts, 1)
            nc.gpsimd.memset(U[:, 0, 0:1], 0.0).then_inc(u_pool, 2)
            nc.gpsimd.memset(U[:, 0, 1:2], 0.0).then_inc(moe_L2, 1)
            nc.gpsimd.memset(U[:, 0, 2:3], 0.0).then_inc(moe_out, 1)
            for par in range(MBUF):
                nc.gpsimd.memset(U[:, 0, 3 + par:4 + par], 0.0).then_inc(s_mo[par], 16)
            nc.gpsimd.iota(iota_e, pattern=[[1, EXPERTS]], base=0, channel_multiplier=0,
                           allow_small_or_imprecise_dtypes=True).then_inc(consts, 1)
            nc.gpsimd.iota(small[:, 800:802], pattern=[[P, 2]], base=0, channel_multiplier=1,
                           allow_small_or_imprecise_dtypes=True).then_inc(consts, 1)
            pool.wait_ge(pchain, 4)
            tv = tri.rearrange("p (g h) -> p g h", g=GROUPS)
            nc.gpsimd.affine_select(out=tv, in_=tv, compare_op=ALU.is_gt, fill=0.0, base=0,
                                    pattern=[[1, GROUPS], [-1, GROUPS]], channel_multiplier=0)\
                .then_inc(consts, 1)
            nc.gpsimd.affine_select(out=ltri, in_=ltri, compare_op=ALU.is_gt, fill=0.0, base=0,
                                    pattern=[[1, P]], channel_multiplier=-1).then_inc(consts, 1)

            def scatter(k, t):
                pool.indirect_dma_start(xg_d, bass.IndirectOffsetOnAxis(ap=slot[:, k, t:t + 1].bitcast(u32), axis=0),
                                        XN[:, t, :], None).then_inc(scattered, 16)

            def body(it):
                for s in range(SL):
                    c = s + GLEAD - 1
                    if on_gpsimd(it, c):
                        pool.wait_ge(gs_ready, by_gpsimd(it, c) + 1)
                        pool.wait_ge(scan_done, it * SL + c - 3)
                        b = c // PAIRS % NBATCH
                        nc.gpsimd.tensor_tensor(U[:, c % 4, :], GS[:, c // 2 % 2, :], B2[:, b * L:(b + 1) * L],
                                                ALU.mult).then_inc(u_pool, 1)

            def add_shared(first, last):
                for t in range(first, last):
                    pool.wait_ge(sh_copied, t + 1)
                    nc.gpsimd.tensor_tensor(X[:, t, :], shared_out[t % 2], X[:, t, :], ALU.add).then_inc(sh_ready, 1)

            add_shared(0, TT - 4)
            pool.wait_ge(slots_ready, 1)
            pool.wait_ge(zeros_stored, 16 * ((NXT + 7) // 8))
            for k in range(TOPK):
                for t in range(TT):
                    scatter(k, t)
                if k == 0:
                    add_shared(TT - 4, TT)
            for it in range(PRE):
                body(it)
            with pool.Fori(PRE, BLK - 1) as it:
                body(it)
            body(BLK - 1)
            for par in range(MBUF):
                pool.wait_ge(s_mo[par], 16 * (NPAIR // MBUF + 1))
            pool.wait_ge(s_mx[(NPAIR + 1) % MBUF], 48 * ((NPAIR + 1) // MBUF + 1))
            pool.wait_ge(s_mx[NPAIR % MBUF], 48 * (NPAIR // MBUF + 1))
            for t in range(TT):
                for k in range(TOPK):
                    n = t * TOPK + k
                    pool.wait_ge(comb, at_least_0(n - RING + 1))
                    pool.indirect_dma_start(row(n), None, yg_d,
                                            bass.IndirectOffsetOnAxis(ap=slot[:, k, t:t + 1].bitcast(u32), axis=0))\
                        .then_inc(s_g[n % RING], 16)

        @block.scalar
        def _(act):
            for ln in range(2):
                act.wait_ge(stats_ready, ln + 1)
                nc.scalar.activation(rstd[:, :], rtmp[:, 0, :], ACT.Sqrt).then_inc(sqrt_ready, 1)
            for q in range(8):
                act.wait_ge(job_done, JN["xnT", q] + 1)
                h, g4 = q % 2, q // 2
                nc.scalar.copy(xnT[:, h, 512 * g4:512 * g4 + 512], ps[:, job_bank(JN["xnT", q]), :])\
                    .then_inc(act_evac, 1)
            for q in range(2):
                n = JN["logit", q]
                act.wait_ge(job_done, n + 1)
                nc.scalar.activation(U[:, 2, q * 512:(q + 1) * 512], ps[:, job_bank(n), :], ACT.Exp, scale=-1.0)\
                    .then_inc(act_evac, 1)
            act.wait_ge(w_in, 80)
            nc.scalar.activation(Aneg[:, 0:P], Aneg[:, 0:P], ACT.Exp).then_inc(a_exp, 1)
            for q in range(4):
                n = JN["dpre", q]
                act.wait_ge(job_done, n + 1)
                nc.scalar.copy(dpre[:, 512 * q:512 * q + 512], ps[:, job_bank(n), :]).then_inc(act_evac, 1)
            def shared_steps(first, last):
                for s in range(first, last):
                    q, i = s // 8, s % 8
                    if i < 4:
                        n = 4 * q + i
                        act.wait_ge(up_mm, n + 1)
                        nc.scalar.activation(ps[:, s % 2, :], ps[:, s % 2, :], ACT.Relu).then_inc(up_relu, 1)
                        act.wait_ge(up_relu, n + 1)
                        nc.scalar.activation(hid[i], ps[:, s % 2, :], ACT.Square).then_inc(up_sq, 1)
                    else:
                        t = 4 * q + i - 4
                        act.wait_ge(sh_mm, t + 1)
                        act.wait_ge(sh_ready, at_least_0(t - 1))
                        nc.scalar.copy(shared_out[t % 2], ps[:, s % 2, 0:D]).then_inc(sh_copied, 1)

            shared_steps(0, SH_CUT[1])
            for q in range(4):
                act.wait_ge(z_ready, q + 1)
                nc.scalar.activation(e_t, e_t, ACT.Exp).then_inc(e_ready, 1)
                act.wait_ge(e_ready, 2 * q + 1)
                nc.scalar.activation(l_t, e_t, ACT.Ln, bias=1.0).then_inc(e_ready, 1)
                for kind in range(2):
                    act.wait_ge(dt_ready_p, 2 * q + kind + 1)
                    act.wait_ge(parts_stored, 16 * STORED[q])
                    nc.scalar.copy(prt3[:, 2 * kind, :], dtg[:, kind, :]).then_inc(part1_ready, 1)
                for kind in range(2):
                    act.wait_ge(part2_ready, 2 * q + kind + 1)
                    nc.scalar.copy(prt3[:, 2 * kind + 1, :], res[:, kind, :]).then_inc(part1_ready, 1)
                if q == 0:
                    shared_steps(SH_CUT[1], SH_CUT[2])

            act.wait_ge(xs_stored, 16)

            def decay(it, c):
                b, pair = c // PAIRS % NBATCH, c % PAIRS
                if pair == 0:
                    act.wait_ge(s_parts[b], (it + c // SL + 1) * PLOAD)
                act.wait_ge(scan_done, at_least_0(it * SL + c - 3))
                for k in range(2):
                    act.wait_ge(dt_bcast, 2 * (it * SL + c) + k + 1)
                    nc.scalar.activation(AD[:, c % 4, 512 * k:512 * k + 512], ps[:, k, :], ACT.Exp,
                                         scale=Acur[:, b, pair:pair + 1]).then_inc(a_ready, 1)

            def body(it, moe):
                for s in range(SL):
                    if moe and s % 2 == 0 and s // 2 < MPI:
                        act.wait_ge(moe_T, (it - PRE) * MPI + s // 2 + 1)
                        nc.scalar.copy(XT[:, :, :, :].rearrange("p u k t -> p (u k t)"), ps[:, 7, :]).then_inc(moe_xT, 1)
                    if moe and s % 2 == 1 and s // 2 < MPI:
                        act.wait_ge(moe_L1, (it - PRE) * MPI + s // 2 + 1)
                        nc.scalar.activation(RL[:, :, :], ps[:, 4, 0:2 * P].rearrange("p (u t) -> p u t", u=2), ACT.Relu)\
                            .then_inc(moe_relu, 1)
                    decay(it, s + DLEAD)
                    if s % 2 == 1:
                        f = (s % GRP) // 2
                        evac_fill((it * 4 + s // GRP - 1) * NFILL + f, f)
                    c = s + GLEAD
                    if on_gpsimd(it, c):
                        act.wait_ge(g_bcast, it * SL + c + 1)
                        act.wait_ge(u_pool, by_gpsimd(it, c) + 1)
                        nc.scalar.copy(GS[:, c // 2 % 2, :].rearrange("p (a c) -> p a c", a=2), ps[:, 2:4, :])\
                            .then_inc(gs_ready, 1)

            def evac_fill(F, f):
                if isinstance(F, int) and F < 0:
                    return
                act.wait_ge(y_filled, F + 1)
                act.wait_ge(s_ys[f % 2], at_least_0(32 * (F // 2) if isinstance(F, int) else (F - f % 2) * 16))
                nc.scalar.copy(YS[:, f % 2, :], ps[:, 6, :]).then_inc(y_evac, 1)

            for c in range(DLEAD):
                decay(0, c)
            for it in range(PRE):
                body(it, False)
            with act.Fori(PRE, BLK - 1) as it:
                body(it, True)
            body(BLK - 1, False)
            for f in range(NFILL):
                evac_fill((BLK * 4 - 1) * NFILL + f, f)

        @block.vector
        def _(dve):
            count = [0]

            def link(ins):
                count[0] += 1
                ins.then_inc(chain, 1)
                dve.wait_ge(chain, count[0])

            V = nc.vector

            def layernorm(src, dst, ln):
                for k in range(TT):
                    if ln == 0 and k == 0:
                        dve.wait_ge(x_in, 64)
                    ins = V.bn_stats(st6[:, k, :], src[:, k, :])
                    if k == TT - 1:
                        link(ins)
                for k in range(TT):
                    ins = V.bn_aggr(mv[:, k, :], st6[:, k, :])
                link(ins)
                V.tensor_scalar(rtmp[:, 0, :], mv[:, :, 1], EPS, None, ALU.add).then_inc(stats_ready, 1)
                dve.wait_ge(sqrt_ready, ln + 1)
                link(V.reciprocal(rstd[:, :], rstd[:, :]))
                link(V.tensor_tensor(rtmp[:, 1, :], rstd[:, :], rstd[:, :], ALU.mult))
                link(V.tensor_tensor(rtmp[:, 1, :], rtmp[:, 1, :], rtmp[:, 0, :], ALU.mult))
                link(V.tensor_scalar(rtmp[:, 1, :], rtmp[:, 1, :], -0.5, 1.5, ALU.mult, ALU.add))
                link(V.tensor_tensor(rstd[:, :], rstd[:, :], rtmp[:, 1, :], ALU.mult))
                for k in range(TT):
                    ins = V.tensor_scalar(dst[:, k, :], src[:, k, :], mv[:, k, 0:1], rstd[:, k:k + 1],
                                          ALU.subtract, ALU.mult)
                ins.then_inc(xn_ready, 1)
                dve.wait_ge(xn_ready, ln + 1)

            layernorm(X, XN, 0)
            layernorm(XN, XN2, 1)
            dve.wait_ge(act_evac, evac_no(JN["logit", 1]))
            dve.wait_ge(bias_in, 16)
            dve.wait_ge(consts, 9)
            t8 = lambda a: a.rearrange("p (g e) -> p g e", e=8)
            t64 = lambda a: a.rearrange("p (t e) -> p t e", e=EXPERTS)
            g1, g2, g3, gs, pen = (small[:, 128 * n:128 * n + 128] for n in range(5))
            link(V.tensor_scalar(sc, sc, 1.0, None, ALU.add))
            link(V.reciprocal(sc, sc))
            link(V.tensor_tensor(t64(scb), t64(sc), bias_b.unsqueeze(1).broadcast_to((P, TT, EXPERTS)), ALU.add))
            dve.wait_ge(w_in, 80)
            for q in range(8):
                n = JN["xn2T", q]
                dve.wait_ge(job_done, n + 1)
                h, g4 = q % 2, q // 2
                V.tensor_scalar(xn2T[:, h, 512 * g4:512 * g4 + 512], ps[:, job_bank(n), :], vec[:, h, 0:1], vec[:, h, 1:2],
                                ALU.mult, ALU.add).then_inc(dve_evac, 1)
            for q in range(4):
                n = JN["B", q]
                dve.wait_ge(job_done, n + 1)
                V.tensor_copy(B2[:, 512 * q:512 * q + 512], ps[:, job_bank(n), :]).then_inc(dve_evac, 1)
            dve.wait_ge(a_exp, 1)
            V.tensor_scalar(Aneg[:, 0:P], Aneg[:, 0:P], -1.0, None, ALU.mult).then_inc(aneg_ready, 1)
            V.memset(Aneg[:, P:], 0.0).then_inc(aneg_ready, 1)

            bc8 = lambda a: a.unsqueeze(2).broadcast_to((P, P, 8))
            link(V.tensor_reduce(g1, t8(scb), AX.X, ALU.max))
            link(V.tensor_tensor(t8(ra), t8(scb), bc8(g1), ALU.is_equal))
            V.tensor_reduce(g2, t8(ra), AX.X, ALU.add)
            link(V.scalar_tensor_tensor(rb, ra, -BIG, scb, ALU.mult, ALU.add))
            V.tensor_reduce(g3, t8(rb), AX.X, ALU.max)
            link(V.tensor_scalar(g2, g2, 1.5, -BIG, ALU.is_lt, ALU.mult))
            link(V.tensor_tensor(g2, g2, g1, ALU.add))
            link(V.tensor_tensor(g3, g3, g2, ALU.max))
            link(V.tensor_tensor(gs, g1, g3, ALU.add))
            v3 = lambda a: a.rearrange("p (t g h) -> p t g h", g=GROUPS, h=GROUPS)
            gsv = gs.rearrange("p (t g) -> p t g", g=GROUPS)
            gh = gsv.unsqueeze(2).broadcast_to((P, TT, GROUPS, GROUPS))
            gg = gsv.unsqueeze(3).broadcast_to((P, TT, GROUPS, GROUPS))
            link(V.tensor_tensor(v3(rb), gh, gg, ALU.is_equal))
            link(V.tensor_tensor(t64(rb), t64(rb), tri.unsqueeze(1).broadcast_to((P, TT, 64)), ALU.mult))
            link(V.tensor_tensor(v3(ra), gh, gg, ALU.is_gt))
            link(V.tensor_tensor(ra, ra, rb, ALU.add))
            link(V.tensor_reduce(g2, t8(ra), AX.X, ALU.add))
            link(V.tensor_scalar(pen, g2, TOPG - 0.5, BIG, ALU.is_lt, ALU.mult))
            link(V.tensor_scalar(pen, pen, -BIG, None, ALU.add))
            link(V.tensor_tensor(t8(scb), t8(scb), bc8(pen), ALU.add))
            top = g1.rearrange("p (t e) -> p t e", e=8)
            idx = g2.bitcast(u32).rearrange("p (t e) -> p t e", e=8)
            idf = g3.rearrange("p (t e) -> p t e", e=8)
            for t in range(TT):
                ins = V.max(top[:, t, :], t64(scb)[:, t, :])
            link(ins)
            for t in range(TT):
                ins = V.max_index(idx[:, t, :], top[:, t, :], t64(scb)[:, t, :])
            link(ins)
            link(V.tensor_copy(idf, idx))
            iob = iota_e.unsqueeze(1).broadcast_to((P, TT, EXPERTS))
            for k in range(TOPK):
                V.tensor_tensor(t64(OH[k]), iob, idf[:, :, k:k + 1].broadcast_to((P, TT, EXPERTS)),
                                ALU.is_equal).then_inc(oh_ready, 1)
                dve.wait_ge(oh_ready, k + 1)
                link(V.tensor_tensor(ra, OH[k], sc, ALU.mult))
                link(V.tensor_reduce(wn[:, :, k], t64(ra), AX.X, ALU.add))
            dve.wait_ge(zeros_stored, 16 * ((NXT + 7) // 8))
            for b in range(2):
                n = JN["C", b]
                dve.wait_ge(job_done, n + 1)
                V.tensor_copy(CB[0:N, b, :, 0], ps[0:N, job_bank(n), 0:PERIOD])
                V.tensor_copy(CB[N:P, b, :, 1], ps[N:P, job_bank(n), 0:PERIOD]).then_inc(dve_evac, 1)
            wsum = small[:, 640:656]
            link(V.tensor_reduce(wsum, wn[:, :, :], AX.X, ALU.add))
            link(V.tensor_scalar(wsum, wsum, 1e-20, None, ALU.add))
            link(V.reciprocal(wsum, wsum))
            link(V.tensor_scalar(wsum, wsum, SCALE, None, ALU.mult))
            link(V.tensor_tensor(wn[:, :, :], wn[:, :, :], wsum.unsqueeze(2).broadcast_to((P, TT, TOPK)), ALU.mult))
            for q in range(4):
                n = JN["prefix", q]
                dve.wait_ge(job_done, n + 1)
                dst = pos if q < 2 else tot
                V.tensor_copy(dst[:, 512 * (q % 2):512 * (q % 2) + 512], ps[:, job_bank(n), :]).then_inc(dve_evac, 1)
            dve.wait_ge(dve_evac, evac_no(JN["prefix", 3]))
            run = t64(rb)
            link(V.tensor_copy(run[:, 0, :], t64(tot)[:, 0, :]))
            for t in range(1, TT):
                link(V.tensor_tensor(run[:, t, :], run[:, t - 1, :], t64(tot)[:, t, :], ALU.add))
            link(V.tensor_tensor(t64(pos)[:, 1:, :], t64(pos)[:, 1:, :], run[:, :TT - 1, :], ALU.add))
            nt = rc[:, 0:64]
            nti = rc[:, 64:128].bitcast(i32)
            incl = rc[:, 128:192]
            one = rc[:, 192:256]
            V.memset(one, 1.0)
            link(V.tensor_scalar(nt, run[:, TT - 1, :], float(P - 1), None, ALU.add))
            link(V.tensor_copy(nti, nt))
            link(V.tensor_scalar(nti, nti, 7, None, ALU.logical_shift_right))
            link(V.tensor_copy(nt, nti))
            link(V.tensor_tensor_scan(incl, one, nt, 0.0, ALU.mult, ALU.add))
            link(V.tensor_tensor(nt, incl, nt, ALU.subtract))
            link(V.tensor_scalar(nt, nt, float(P), None, ALU.mult))
            link(V.tensor_tensor(t64(pos), t64(pos), nt.unsqueeze(1).broadcast_to((P, TT, EXPERTS)), ALU.add))
            for c in range(2):
                link(V.tensor_scalar(one, incl, small[:, 800 + c:801 + c], None, ALU.is_le))
                link(V.tensor_reduce(small[:, 810 + c:811 + c], one, AX.X, ALU.add))
            link(V.tensor_scalar(small[:, 810:812], small[:, 810:812], float(EXPERTS - 1), None, ALU.min))
            V.tensor_copy(mapv[:, :], small[:, 810:812]).then_inc(map_ready, 1)
            for k in range(TOPK):
                link(V.tensor_tensor(ra, OH[k], pos, ALU.mult))
                link(V.tensor_reduce(rc[:, 256 + 16 * k:272 + 16 * k], t64(ra), AX.X, ALU.add))
            V.tensor_copy(slot[:, :, :], rc[:, 256:256 + 96].rearrange("p (k t) -> p k t", k=TOPK))\
                .then_inc(slots_ready, 1)

            for q in range(4):
                h, b = q // 2, q % 2
                for c in range(2):
                    n = JN["dt", 2 * q + c]
                    dve.wait_ge(job_done, n + 1)
                    ins = V.tensor_scalar(z_t[:, 512 * c:512 * c + 512], ps[:, job_bank(n), :], vec[:, h, 2:3], None, ALU.add)
                    ins.then_inc(dve_evac, 1)
                dve.wait_ge(dve_evac, evac_no(n))
                V.scalar_tensor_tensor(e_t, z_t, -1.0, z_t, ALU.mult, ALU.min).then_inc(z_ready, 1)
                dve.wait_ge(e_ready, 2 * q + 2)
                link(V.tensor_scalar(u_t, e_t, 1.0, None, ALU.add))
                link(V.scalar_tensor_tensor(u_t, u_t, -1.0, e_t, ALU.add, ALU.subtract))
                link(V.tensor_tensor(l_t, l_t, u_t, ALU.subtract))
                V.scalar_tensor_tensor(dtg[:, 0, :], z_t, 0.0, l_t, ALU.max, ALU.add).then_inc(dt_ready_p, 1)
                dve.wait_ge(dt_ready_p, 2 * q + 1)
                V.tensor_tensor(dtg[:, 1, :], dtg[:, 0, :], xn2T[:, h, b * L:(b + 1) * L], ALU.mult)\
                    .then_inc(dt_ready_p, 1)
                for kind in range(2):
                    dve.wait_ge(part1_ready, 4 * q + kind + 1)
                    dve.wait_ge(dt_ready_p, 2 * q + kind + 1)
                    V.tensor_tensor(res[:, kind, :], dtg[:, kind, :], prt3[:, 2 * kind, :], ALU.subtract)\
                        .then_inc(part2_ready, 1)
                for kind in range(2):
                    dve.wait_ge(part1_ready, 4 * q + 2 + kind + 1)
                    dve.wait_ge(parts_stored, 16 * STORED[q])
                    V.tensor_tensor(prt[:, kind, :], res[:, kind, :], prt3[:, 2 * kind + 1, :], ALU.subtract)\
                        .then_inc(split_ready, 1)

            dve.wait_ge(split_ready, 8)
            dve.wait_ge(slots_ready, 1)

            def product(it, c):
                b = c // PAIRS % NBATCH
                dve.wait_ge(g_bcast, it * SL + c + 1)
                if two_g(it, c):
                    dve.wait_ge(scan_done, at_least_0(it * SL + c - 3))
                V.tensor_tensor(U[:, c % 4, :].rearrange("p (a c) -> p a c", a=2), ps[:, g_bank(it, c):g_bank(it, c) + 2, :],
                                B2[:, b * L:(b + 1) * L].rearrange("p (a c) -> p a c", a=2), ALU.mult)\
                    .then_inc(g_dve, 1)

            def scan(it, s):
                if isinstance(it, int) and it * SL + s == GRP:
                    dve.wait_ge(parts_stored, 16 * (24 + 12))
                if s % GRP == 0:
                    dve.wait_ge(y_filled, at_least_0((it * 4 + s // GRP - 1) * NFILL))
                if on_gpsimd(it, s):
                    dve.wait_ge(u_pool, by_gpsimd(it, s) + 3)
                else:
                    dve.wait_ge(g_dve, by_vector(it, s) + 1)
                dve.wait_ge(a_ready, 2 * (it * SL + s + 1))
                V.tensor_tensor_scan(H[:, (s // GRP % 2) * GRP + s % GRP, :],
                                     AD[:, s % 4, :], U[:, s % 4, :], 0.0, ALU.mult, ALU.add).then_inc(scan_done, 1)

            def body(it, moe):
                for s in range(SL):
                    if s % 2 == 0:
                        scan(it, s)
                        scan(it, s + 1)
                    j = s // 2
                    m = (it - PRE) * MPI + j
                    if not on_gpsimd(it, s + GLEAD):
                        product(it, s + GLEAD)
                    if moe and s % 2 == 1 and 1 <= j <= MPI:
                        dve.wait_ge(moe_L2, m + 1)
                        dve.wait_ge(s_mo[(j - 1) % MBUF], (it - PRE) * (16 * MPI // MBUF) + (j - 1) // MBUF * 16 + 16)
                        V.tensor_copy(YO[:, (j - 1) % MBUF, :, :].rearrange("p u d -> p (u d)"), ps[:, 5, :])\
                            .then_inc(moe_out, 1)
                    if moe and s % 2 == 1 and j < MPI:
                        dve.wait_ge(moe_relu, m + 1)
                        V.tensor_tensor(AS[:, :, :], RL[:, :, :], RL[:, :, :], ALU.mult).then_inc(moe_sq, 1)
                    if isinstance(it, int) and it == BLK - 1 and s >= 1:
                        for n in range(TT * TOPK * (s - 1) // (SL - 1), TT * TOPK * s // (SL - 1)):
                            combine(n)

            def combine(n):
                t, k = n // TOPK, n % TOPK
                dve.wait_ge(s_g[n % RING], 16 * (n // RING + 1))
                if n:
                    dve.wait_ge(comb, n)
                else:
                    dve.wait_ge(x_again, 16)
                V.scalar_tensor_tensor(XN[:, t, :], row(n), wn[:, t, k:k + 1], XN[:, t, :], ALU.mult, ALU.add)\
                    .then_inc(comb, 1)

            for c in range(GLEAD):
                product(0, c)
            for it in range(PRE):
                body(it, False)
            with dve.Fori(PRE, BLK - 1) as it:
                body(it, True)
            body(BLK - 1, False)

            for h in range(2):
                dve.wait_ge(s_yT, 16 * (h + 1))
                for b in range(2):
                    yv = H[:, 4 + 2 * h + b, :].rearrange("p (r c) -> p r c", r=PERIOD)
                    xv = xnT[:, h, b * L:(b + 1) * L].rearrange("p (c r) -> p r c", r=PERIOD)
                    zv = H[:, 2 * h + b, :].rearrange("p (c r) -> p r c", r=PERIOD)
                    V.scalar_tensor_tensor(zv, xv, vec[:, h, 3:4], yv, ALU.mult, ALU.add).then_inc(z2_ready, 1)
            dve.wait_ge(comb, TT * TOPK)
            for t in range(TT):
                dve.wait_ge(fin_mm, t + 1)
                if t < 2:
                    dve.wait_ge(s_mo[t % 2], 16 * (NPAIR // MBUF + 1))
                else:
                    dve.wait_ge(s_os[t % 2], 16 * (t // 2))
                V.tensor_tensor(YO[:, t % 2, 0, :], ps[:, 2 + t % 4, 0:D], XN[:, t, :], ALU.add)\
                    .then_inc(out_ready, 1)

        @block.tensor
        def _(pe):
            mm = nc.tensor.matmul

            def shared_step(s):
                q, i = s // 8, s % 8
                o = ps[:, s % 2, :]
                if i < 2:
                    pe.wait_ge(sh_copied, at_least_0(4 * q - 2 + i + 1))
                elif i < 6:
                    pe.wait_ge(up_sq, 4 * q + i - 1)
                else:
                    pe.wait_ge(sh_copied, 4 * q + i - 5)
                if i < 4:
                    for k in range(2):
                        ins = nc.tensor.matmul(o, wup[:, k, i * P:(i + 1) * P], xnT[:, k, 512 * q:512 * q + 512],
                                               start=(k == 0), stop=(k == 1))
                    ins.then_inc(up_mm, 1)
                else:
                    pe.wait_ge(up_sq, 4 * q + 4)
                    for k in range(4):
                        ins = nc.tensor.matmul(o[:, 0:D], hid[k][:, (i - 4) * P:(i - 3) * P], wdn[:, k, :],
                                               start=(k == 0), stop=(k == 3))
                    ins.then_inc(sh_mm, 1)

            for n, (kind, q, _) in enumerate(JOBS):
                if (kind, q) == ("prefix", 0):
                    pe.wait_ge(wsh_in, 32)
                    pe.wait_ge(act_evac, evac_no(JN["dpre", 3]))
                    for s in range(SH_CUT[0]):
                        shared_step(s)
                if (kind, q) == ("dt", 6):
                    for s in range(SH_CUT[0], 2 * TT):
                        shared_step(s)
                bank = ps[:, job_bank(n), :]
                last = n - 8 if n < 32 else n - 6
                if n >= 8 and JOBS[last][2] == "act":
                    pe.wait_ge(act_evac, evac_no(last))
                elif n >= 8:
                    pe.wait_ge(dve_evac, evac_no(last))
                if kind in ("xnT", "xn2T"):
                    if q == 0:
                        pe.wait_ge(consts, 1)
                        pe.wait_ge(xn_ready, 1 if kind == "xnT" else 2)
                    src = XN if kind == "xnT" else XN2
                    h, g4 = q % 2, q // 2
                    for j in range(4):
                        ins = nc.tensor.transpose(bank[:, j * P:(j + 1) * P], src[:, 4 * g4 + j, h * P:(h + 1) * P],
                                                  ident[:, :])
                elif kind == "logit":
                    if q == 0:
                        pe.wait_ge(w_in, 80)
                        pe.wait_ge(act_evac, 8)
                    for j in range(8):
                        t = 8 * q + j
                        for k in range(2):
                            ins = mm(bank[:, j * 64:(j + 1) * 64], xnT[:, k, t * P:(t + 1) * P], Wgate[:, k, :],
                                     start=(k == 0), stop=(k == 1))
                elif kind in ("B", "C", "dpre"):
                    if (kind, q) == ("B", 0):
                        pe.wait_ge(dve_evac, 8)
                    m0 = {"dpre": 0, "B": P, "C": 2 * P}[kind]
                    for k in range(2):
                        if kind == "C":
                            ins = mm(bank[:, 0:PERIOD], Wproj[:, k, m0:m0 + P], xn2T[:, k, q * L:q * L + PERIOD],
                                     start=(k == 0), stop=(k == 1))
                        else:
                            ins = mm(bank, Wproj[:, k, m0:m0 + P], xn2T[:, k, 512 * q:512 * q + 512],
                                     start=(k == 0), stop=(k == 1))
                elif kind == "dt":
                    if q == 0:
                        pe.wait_ge(act_evac, evac_no(JN["dpre", 3]))
                    h, tq = q // 4, q % 4
                    ins = mm(bank, Wdt[:, h * P:(h + 1) * P], dpre[:, 512 * tq:512 * tq + 512], start=True, stop=True)
                else:
                    if q == 0:
                        pe.wait_ge(oh_ready, TOPK)
                        pe.wait_ge(consts, 9)
                    for k in range(TOPK):
                        ins = mm(bank, ltri if q < 2 else onesb, OH[k][:, 512 * (q % 2):512 * (q % 2) + 512],
                                 start=(k == 0), stop=(k == TOPK - 1))
                ins.then_inc(job_done, 1)
            pe.wait_ge(dve_evac, evac_no(JN["dt", 7]))
            pe.wait_ge(act_evac, evac_no(JN["dpre", 3]))

            def y_quarter(f, s, b, qq, last):
                hb = H[:, (s // GRP % 2) * GRP:(s // GRP % 2) * GRP + GRP, :]\
                    .rearrange("p g (c r) -> p g c r", r=PERIOD)
                for j in range(4):
                    r = f * 16 + j * 4 + qq
                    o = ps[32 * j:32 * j + 32, 6, :].rearrange("p (g a c) -> p g a c", g=GRP, a=4)[:, :, qq, :]
                    ins = mm(o, CB[:, b, r, :], hb[:, :, :, r], start=True, stop=True)
                if last:
                    ins.then_inc(y_filled, 1)

            def bcast_dt(it, c):
                b, pair = c // PAIRS % NBATCH, c % PAIRS
                if pair == 0:
                    pe.wait_ge(s_parts[b], (it + c // SL + 1) * PLOAD)
                for k in range(2):
                    pe.wait_ge(a_ready, at_least_0(2 * (it * SL + c - 1) + k + 1))
                    mm(ps[:, k, :], sel[:, pair, :], PD[:, b, 512 * k:512 * k + 512],
                       start=True, stop=True).then_inc(dt_bcast, 1)

            def bcast_g(it, c):
                b, pair = c // PAIRS % NBATCH, c % PAIRS
                if pair == 0:
                    pe.wait_ge(s_parts[b], (it + c // SL + 1) * PLOAD)
                if two_g(it, c) and two_g(it, c - 1) and two_g(it, c - 2):
                    pe.wait_ge(g_dve, at_least_0(by_vector(it, c - 1)))
                elif on_gpsimd(it, c - 1):
                    pe.wait_ge(gs_ready, by_gpsimd(it, c))
                else:
                    pe.wait_ge(g_dve, by_vector(it, c))
                if isinstance(it, int) and it * SL + c == LATE:
                    pe.wait_ge(moe_out, NPAIR + 1)
                gb = g_bank(it, c)
                for k in range(2):
                    ins = mm(ps[:, gb + k, :], sel[:, pair, :], PG[:, b, 512 * k:512 * k + 512],
                             start=True, stop=True)
                ins.then_inc(g_bcast, 1)

            def body(it, moe):
                for s in range(SL):
                    j = s // 2
                    m = (it - PRE) * MPI + j
                    par = j % MBUF
                    if moe and s % 2 == 0 and j < MPI:
                        pe.wait_ge(s_mx[par], (m - par) * 16 + 48)
                        for n in range(4):
                            ins = nc.tensor.transpose(ps[:, 7, n * P:(n + 1) * P],
                                                      XG[:, par, n // 2, n % 2 * P:(n % 2 + 1) * P], ident[:, :])
                        ins.then_inc(moe_T, 1)
                    if moe and s % 2 == 1 and j < MPI:
                        pe.wait_ge(moe_xT, m + 1)
                        for u in range(2):
                            for k in range(2):
                                ins = mm(ps[:, 4, u * P:(u + 1) * P], W1[:, par, u, k, :], XT[:, u, k, :],
                                         start=(k == 0), stop=(k == 1))
                        ins.then_inc(moe_L1, 1)
                    bcast_dt(it, s + DLEAD)
                    Fg = it * 4 + s // GRP - 1
                    if not (isinstance(Fg, int) and Fg < 0):
                        yb, f, hf = (s - GRP) % SL // PAIRS, (s % GRP) // 2, s % 2
                        if (f, hf) == (0, 0):
                            pe.wait_ge(scan_done, (Fg + 1) * GRP)
                        if hf == 0:
                            pe.wait_ge(y_evac, Fg * NFILL + f)
                        y_quarter(f, (s - GRP) % SL, yb, 2 * hf, False)
                        y_quarter(f, (s - GRP) % SL, yb, 2 * hf + 1, hf == 1)
                    if moe and s % 2 == 0 and 1 <= j <= MPI:
                        pe.wait_ge(moe_sq, m)
                        pe.wait_ge(moe_out, m)
                        for u in range(2):
                            ins = mm(ps[:, 5, u * D:(u + 1) * D], AS[:, u, :], W2[:, (j - 1) % MBUF, u, :],
                                     start=True, stop=True)
                        ins.then_inc(moe_L2, 1)
                    bcast_g(it, s + GLEAD)

            for c in range(GLEAD):
                bcast_g(0, c)
            for c in range(DLEAD):
                bcast_dt(0, c)
            for it in range(PRE):
                body(it, False)
            with pe.Fori(PRE, BLK - 1) as it:
                body(it, True)
            body(BLK - 1, False)
            for f in range(NFILL):
                if f == 0:
                    pe.wait_ge(scan_done, BLK * SL)
                pe.wait_ge(y_evac, at_least_0((BLK * 4 - 1) * NFILL + f))
                for qq in range(4):
                    y_quarter(f, SL - GRP, 1, qq, qq == 3)

            pe.wait_ge(g_dve, by_vector(BLK, GLEAD))
            pe.wait_ge(wend_in, 16)
            pe.wait_ge(z2_ready, 4)
            for t in range(TT):
                pe.wait_ge(out_ready, at_least_0(t - 3))
                b = t // 8
                for h in range(2):
                    ins = mm(ps[:, 2 + t % 4, 0:D], H[:, 2 * h + b, (t % 8) * P:(t % 8 + 1) * P], wo[:, h, :],
                             start=(h == 0), stop=(h == 1))
                ins.then_inc(fin_mm, 1)


def kernel(**inputs):
    import concourse.bacc as _bacc
    from concourse.bass_utils import run_bass_kernel_spmd as _run

    a = {k.replace("L0_attn_", "").replace("L0_ffn_", ""): np.asarray(v) for k, v in inputs.items()}
    wp = a["x_proj_w"]
    wp = np.concatenate([wp[:RANK], wp[RANK:RANK + N], wp[RANK:RANK + N], wp[RANK + N:], wp[RANK + N:]])

    def rows(m):
        return m.reshape(2, P, -1).transpose(1, 0, 2)

    arrays = {
        "x_dram": a["x"].reshape(T, D),
        "xprojT_dram": rows(wp.T),
        "dtT_dram": a["dt_proj_w"].T,
        "vecs_dram": np.stack([a["norm_w"], a["norm_b"], a["dt_proj_b"], a["D_param"]]).reshape(4, 2, P).transpose(2, 1, 0),
        "A_l_dram": a["A_log"].reshape(P, 2, N).transpose(1, 2, 0).reshape(P, P),
        "outT_dram": rows(a["out_proj_w"].T),
        "gateT_dram": rows(a["gate_w"].T),
        "gbias_dram": a["gate_bias"],
        "w_up_dram": a["w_up_shared"],
        "w_down_dram": a["w_down_shared"],
        "w_exp_dram": np.concatenate([a["w1_experts"].reshape(EXPERTS, 2, P, INTER).transpose(0, 2, 1, 3)
                                      .reshape(EXPERTS, P, 2 * INTER), a["w2_experts"]], axis=2),
    }
    arrays = {k: np.ascontiguousarray(v) for k, v in arrays.items()}
    nc = _bacc.Bacc("TRN2", target_bir_lowering=False, num_devices=1)
    args = [nc.dram_tensor(k, v.shape, mybir.dt.from_np(v.dtype), kind="ExternalInput").ap() for k, v in arrays.items()]
    args.append(nc.dram_tensor("out_dram", (T, D), mybir.dt.float32, kind="ExternalOutput").ap())
    state_space_and_experts(nc, *args)
    r = _run(nc, [arrays], core_ids=[0])
    return r.results[0]["out_dram"].reshape(a["x"].shape)
```
